# Optimizing a Trainium2 kernel written in Bass

```python
import numpy as np
import jax
import jax.numpy as jnp

def _softmax(x, axis=-1):
    return jax.nn.softmax(x, axis=axis)

def _gelu(x):
    return jax.nn.gelu(x, approximate=True)

def _silu(x):
    return jax.nn.silu(x)

def _sigmoid(x):
    return jax.nn.sigmoid(x)

def _layernorm(x, axis=-1, eps=1e-05):
    m = jnp.mean(x, axis=axis, keepdims=True)
    v = jnp.var(x, axis=axis, keepdims=True)
    return (x - m) / jnp.sqrt(v + eps)

def _scatter_add(tgt, idx, src, axis=0):
    return tgt.at[idx].add(src)

def _segment_sum(src, seg, n):
    return jax.ops.segment_sum(src, seg, n)
kernel_name = 'mk_cond_seq_d2_seqx_r8_16bda9'

def setup_inputs(seed: int=0):
    np.random.seed(seed)
    _w = jnp.asarray

    def _rec_inputs():
        import jax
        import jax.numpy as jnp
        _rk = jax.random.key(seed)
        x = 7.22e-05 + 1 * jax.random.normal(jax.random.fold_in(_rk, 1), (4, 256, 256), jnp.float32)
        _lenS = 256 - jax.random.randint(jax.random.fold_in(_rk, 7), (4,), 0, max(1, 256 // 4) + 1, jnp.int32)
        _lenS2 = 256 - jax.random.randint(jax.random.fold_in(_rk, 8), (4,), 0, max(1, 256 // 4) + 1, jnp.int32)
        cond_2048 = 0.0061147 + 1.02565 * jax.random.normal(jax.random.fold_in(_rk, 11), (4, 256), jnp.float32)
        pos_BxS = jnp.broadcast_to(jnp.arange(256, dtype=jnp.int32), (4, 256))
        _validS = jnp.arange(256)[None, :] < _lenS[:, None]
        _validS2 = jnp.arange(256)[None, :] < _lenS2[:, None]
        _causal = jnp.tril(jnp.ones((256, 256), dtype=bool))
        mask_1x1xSxS_ff0 = jnp.where(jnp.ones((1, 1, 256, 256), dtype=bool), 0.0, -1000000000.0).astype(jnp.float32)
        mask_Bx1xSxS_bf1 = jnp.ones((4, 1, 256, 256), dtype=bool)
        return (x, cond_2048, pos_BxS, mask_1x1xSxS_ff0, mask_Bx1xSxS_bf1)
    x, cond_2048, pos_BxS, mask_1x1xSxS_ff0, mask_Bx1xSxS_bf1 = _rec_inputs()

    def _L0_cond_setup():
        import jax, jax.numpy as jnp
        import numpy as np
        B, L, C, H = (2, 256, 256, 16)
        COND = 256
        HID = 4 * C
        LN_EPS = 1e-06

        def _ln(x):
            m = jnp.mean(x, axis=-1, keepdims=True)
            v = jnp.mean((x - m) ** 2, axis=-1, keepdims=True)
            return (x - m) / jnp.sqrt(v + LN_EPS)

        def _gelu_tanh(u):
            c = np.sqrt(2.0 / np.pi).astype(np.float32)
            return 0.5 * u * (1.0 + jnp.tanh(c * (u + 0.044715 * u ** 3)))
        key = jax.random.key(seed)
        ks = jax.random.split(key, 8)
        s = 0.02
        return {'x': jax.random.normal(ks[0], (B, L, C), jnp.float32), 'cond_BD': jax.random.normal(ks[1], (B, COND), jnp.float32), 'attn_bias': jnp.zeros((1, 1, L, L), jnp.float32), 'Wqkv': jax.random.normal(ks[2], (3 * C, C), jnp.float32) * s, 'q_bias': jnp.zeros((C,), jnp.float32), 'v_bias': jnp.zeros((C,), jnp.float32), 'scale_mul_log': jnp.full((1, H, 1, 1), np.log(4.0), jnp.float32), 'Wproj': jax.random.normal(ks[3], (C, C), jnp.float32) * s, 'bproj': jnp.zeros((C,), jnp.float32), 'Wada': jax.random.normal(ks[4], (6 * C, COND), jnp.float32) * s, 'bada': jnp.zeros((6 * C,), jnp.float32), 'Wfc1': jax.random.normal(ks[5], (HID, C), jnp.float32) * s, 'bfc1': jnp.zeros((HID,), jnp.float32), 'Wfc2': jax.random.normal(ks[6], (C, HID), jnp.float32) * s, 'bfc2': jnp.zeros((C,), jnp.float32)}
    _L0_cond_all = _L0_cond_setup()
    _L0_cond_in = {k: v for k, v in _L0_cond_all.items() if k in ('Wqkv', 'q_bias', 'v_bias', 'scale_mul_log', 'Wproj', 'bproj', 'Wada', 'bada', 'Wfc1', 'bfc1', 'Wfc2', 'bfc2')}
    del _L0_cond_all

    def _L1_cond_setup():
        import jax, jax.numpy as jnp
        import numpy as np
        D_MODEL = 256
        D_HEAD = 64
        N_HEADS = D_MODEL // D_HEAD
        EPS_NORM = 1e-06
        EPS_COS = 1e-06
        ROPE_BASE = 10000.0
        NEG_INF = -1e+30

        def _rms_norm(x, scale, eps):
            mean_sq = jnp.mean(jnp.square(x), axis=-1, keepdims=True)
            return x * (scale * jax.lax.rsqrt(mean_sq + eps))

        def _scale_for_cosine_sim(q, k, scale, eps):
            sqrt_scale = jnp.sqrt(scale)
            sq = jnp.sum(jnp.square(q), axis=-1, keepdims=True)
            sk = jnp.sum(jnp.square(k), axis=-1, keepdims=True)
            return (q * (sqrt_scale * jax.lax.rsqrt(sq + eps)), k * (sqrt_scale * jax.lax.rsqrt(sk + eps)))

        def _rope(q, k):
            l, e = (q.shape[-2], q.shape[-1])
            half = e // 2
            inv_freq = 1.0 / ROPE_BASE ** (jnp.arange(0, half, dtype=jnp.float32) / half)
            theta = jnp.arange(l, dtype=jnp.float32)[:, None] * inv_freq[None, :]
            cos, sin = (jnp.cos(theta), jnp.sin(theta))

            def rot(t):
                t1, t2 = (t[..., :half], t[..., half:])
                return jnp.concatenate([t1 * cos - t2 * sin, t1 * sin + t2 * cos], axis=-1)
            return (rot(q), rot(k))
        key = jax.random.key(seed)
        ks = jax.random.split(key, 6)
        n, l = (4, 128)
        x = jax.random.normal(ks[0], (n, l, D_MODEL), dtype=jnp.float32)
        pos = jnp.broadcast_to(jnp.arange(l, dtype=jnp.int32)[None, :], (n, l))
        mask = jnp.ones((n, 1, l, l), dtype=bool)
        cond = jax.random.normal(ks[1], (n, D_MODEL), dtype=jnp.float32)
        norm_w = jax.random.normal(ks[2], (D_MODEL, D_MODEL), dtype=jnp.float32) * 0.02
        qkv_w = jax.random.normal(ks[3], (3 * D_MODEL, D_MODEL), dtype=jnp.float32) * 0.02
        scale = jnp.full((N_HEADS,), 10.0, dtype=jnp.float32)
        out_w = jax.random.normal(ks[4], (D_MODEL, D_MODEL), dtype=jnp.float32) * 0.02
        return {'x': x, 'pos': pos, 'mask': mask, 'cond': cond, 'norm_w': norm_w, 'qkv_w': qkv_w, 'scale': scale, 'out_w': out_w}
    _L1_cond_all = _L1_cond_setup()
    _L1_cond_in = {k: v for k, v in _L1_cond_all.items() if k in ('norm_w', 'qkv_w', 'scale', 'out_w')}
    del _L1_cond_all
    return {'x': x, 'cond_2048': cond_2048, 'pos_BxS': pos_BxS, 'mask_1x1xSxS_ff0': mask_1x1xSxS_ff0, 'mask_Bx1xSxS_bf1': mask_Bx1xSxS_bf1, 'L0_cond_Wqkv': _L0_cond_in['Wqkv'], 'L0_cond_q_bias': _L0_cond_in['q_bias'], 'L0_cond_v_bias': _L0_cond_in['v_bias'], 'L0_cond_scale_mul_log': _L0_cond_in['scale_mul_log'], 'L0_cond_Wproj': _L0_cond_in['Wproj'], 'L0_cond_bproj': _L0_cond_in['bproj'], 'L0_cond_Wada': _L0_cond_in['Wada'], 'L0_cond_bada': _L0_cond_in['bada'], 'L0_cond_Wfc1': _L0_cond_in['Wfc1'], 'L0_cond_bfc1': _L0_cond_in['bfc1'], 'L0_cond_Wfc2': _L0_cond_in['Wfc2'], 'L0_cond_bfc2': _L0_cond_in['bfc2'], 'L1_cond_norm_w': _L1_cond_in['norm_w'], 'L1_cond_qkv_w': _L1_cond_in['qkv_w'], 'L1_cond_scale': _L1_cond_in['scale'], 'L1_cond_out_w': _L1_cond_in['out_w']}

def reference(x, cond_2048, pos_BxS, mask_1x1xSxS_ff0, mask_Bx1xSxS_bf1, L0_cond_Wqkv, L0_cond_q_bias, L0_cond_v_bias, L0_cond_scale_mul_log, L0_cond_Wproj, L0_cond_bproj, L0_cond_Wada, L0_cond_bada, L0_cond_Wfc1, L0_cond_bfc1, L0_cond_Wfc2, L0_cond_bfc2, L1_cond_norm_w, L1_cond_qkv_w, L1_cond_scale, L1_cond_out_w):
    import jax
    import jax.numpy as jnp

    def _L0_cond_ref(x, cond_BD, attn_bias, Wqkv, q_bias, v_bias, scale_mul_log, Wproj, bproj, Wada, bada, Wfc1, bfc1, Wfc2, bfc2):
        import jax, jax.numpy as jnp
        import numpy as np
        B, L, C, H = (2, 256, 256, 16)
        COND = 256
        HID = 4 * C
        LN_EPS = 1e-06

        def _ln(x):
            m = jnp.mean(x, axis=-1, keepdims=True)
            v = jnp.mean((x - m) ** 2, axis=-1, keepdims=True)
            return (x - m) / jnp.sqrt(v + LN_EPS)

        def _gelu_tanh(u):
            c = np.sqrt(2.0 / np.pi).astype(np.float32)
            return 0.5 * u * (1.0 + jnp.tanh(c * (u + 0.044715 * u ** 3)))
        Bs, Lx, Cx = x.shape
        D = Cx // H
        ada = (jax.nn.silu(cond_BD) @ Wada.T + bada).reshape(Bs, 1, 6, Cx)
        gamma1, gamma2, scale1, scale2, shift1, shift2 = [ada[:, :, i, :] for i in range(6)]

        def attn(xin):
            qkv_bias = jnp.concatenate([q_bias, jnp.zeros_like(q_bias), v_bias])
            qkv = (xin @ Wqkv.T + qkv_bias).reshape(Bs, Lx, 3, H, D)
            qkv = jnp.transpose(qkv, (2, 0, 3, 1, 4))
            q, k, v = (qkv[0], qkv[1], qkv[2])
            sm = jnp.exp(jnp.minimum(scale_mul_log, jnp.log(jnp.float32(100.0))))
            qn = q / jnp.maximum(jnp.linalg.norm(q, axis=-1, keepdims=True), 1e-12) * sm
            kn = k / jnp.maximum(jnp.linalg.norm(k, axis=-1, keepdims=True), 1e-12)
            scores = jnp.einsum('bhqd,bhkd->bhqk', qn, kn) + attn_bias
            p = jax.nn.softmax(scores, axis=-1)
            o = jnp.einsum('bhqk,bhkd->bhqd', p, v)
            o = jnp.transpose(o, (0, 2, 1, 3)).reshape(Bs, Lx, Cx)
            return o @ Wproj.T + bproj
        x = x + attn(_ln(x) * (scale1 + 1.0) + shift1) * gamma1
        h = _gelu_tanh((_ln(x) * (scale2 + 1.0) + shift2) @ Wfc1.T + bfc1)
        x = x + (h @ Wfc2.T + bfc2) * gamma2
        return x

    def _L1_cond_ref(x, pos, mask, cond, norm_w, qkv_w, scale, out_w):
        import jax, jax.numpy as jnp
        import numpy as np
        D_MODEL = 256
        D_HEAD = 64
        N_HEADS = D_MODEL // D_HEAD
        EPS_NORM = 1e-06
        EPS_COS = 1e-06
        ROPE_BASE = 10000.0
        NEG_INF = -1e+30

        def _rms_norm(x, scale, eps):
            mean_sq = jnp.mean(jnp.square(x), axis=-1, keepdims=True)
            return x * (scale * jax.lax.rsqrt(mean_sq + eps))

        def _scale_for_cosine_sim(q, k, scale, eps):
            sqrt_scale = jnp.sqrt(scale)
            sq = jnp.sum(jnp.square(q), axis=-1, keepdims=True)
            sk = jnp.sum(jnp.square(k), axis=-1, keepdims=True)
            return (q * (sqrt_scale * jax.lax.rsqrt(sq + eps)), k * (sqrt_scale * jax.lax.rsqrt(sk + eps)))

        def _rope(q, k):
            l, e = (q.shape[-2], q.shape[-1])
            half = e // 2
            inv_freq = 1.0 / ROPE_BASE ** (jnp.arange(0, half, dtype=jnp.float32) / half)
            theta = jnp.arange(l, dtype=jnp.float32)[:, None] * inv_freq[None, :]
            cos, sin = (jnp.cos(theta), jnp.sin(theta))

            def rot(t):
                t1, t2 = (t[..., :half], t[..., half:])
                return jnp.concatenate([t1 * cos - t2 * sin, t1 * sin + t2 * cos], axis=-1)
            return (rot(q), rot(k))
        n, l, d = x.shape
        skip = x
        ada = cond @ norm_w.T + 1.0
        h = _rms_norm(x, ada[:, None, :], EPS_NORM)
        qkv = h @ qkv_w.T
        qkv = qkv.reshape(n, l, 3, N_HEADS, D_HEAD)
        qkv = jnp.transpose(qkv, (2, 0, 3, 1, 4))
        q, k, v = (qkv[0], qkv[1], qkv[2])
        q, k = _scale_for_cosine_sim(q, k, scale[:, None, None], EPS_COS)
        q, k = _rope(q, k)
        scores = jnp.einsum('bhle,bhme->bhlm', q, k)
        scores = jnp.where(mask, scores, NEG_INF)
        attn = jax.nn.softmax(scores, axis=-1)
        o = jnp.einsum('bhlm,bhme->bhle', attn, v)
        o = jnp.transpose(o, (0, 2, 1, 3)).reshape(n, l, d)
        return o @ out_w.T + skip
    x = _L0_cond_ref(x, cond_2048, mask_1x1xSxS_ff0, L0_cond_Wqkv, L0_cond_q_bias, L0_cond_v_bias, L0_cond_scale_mul_log, L0_cond_Wproj, L0_cond_bproj, L0_cond_Wada, L0_cond_bada, L0_cond_Wfc1, L0_cond_bfc1, L0_cond_Wfc2, L0_cond_bfc2)
    x = _L1_cond_ref(x, pos_BxS, mask_Bx1xSxS_bf1, cond_2048, L1_cond_norm_w, L1_cond_qkv_w, L1_cond_scale, L1_cond_out_w)
    return x

_drawn_inputs = setup_inputs


def setup_inputs(seed=0):
    import zlib

    import numpy as np

    out = dict(_drawn_inputs(seed))
    spreads = {'L0_cond_q_bias': (0.0, 0.8),
     'L0_cond_v_bias': (0.0, 0.8),
     'L0_cond_scale_mul_log': (1.3862943649291992, 0.6),
     'L0_cond_bproj': (0.0, 0.373),
     'L0_cond_bada': (0.0, 0.409),
     'L0_cond_bfc1': (0.0, 0.8),
     'L0_cond_bfc2': (0.0, 0.355),
     'L1_cond_scale': (10.0, 0.6)}
    factors = {'L0_cond_Wqkv': 8.0,
     'L0_cond_Wproj': 5.885,
     'L1_cond_norm_w': 6.821,
     'L1_cond_qkv_w': 3.693,
     'L1_cond_out_w': 3.65}
    for name, (base, spread) in spreads.items():
        noise = np.random.default_rng([zlib.crc32(name.encode()), seed]).standard_normal(out[name].shape)
        drawn = base * np.exp(spread * noise) if base else spread * noise
        out[name] = jnp.asarray(drawn.astype(out[name].dtype))
    for name, factor in factors.items():
        out[name] = (out[name] * factor).astype(out[name].dtype)
    return out
```

```python
from contextlib import ExitStack

import numpy as np

import concourse.bass as bass
from concourse import mybir

F32 = mybir.dt.float32
F32R = mybir.dt.float32r
BF16 = mybir.dt.bfloat16
I32 = mybir.dt.int32
ALU = mybir.AluOpType
ACT = mybir.ActivationFunctionType
AX = mybir.AxisListType

P = 128
B, L, C = 4, 256, 256
NT = B * L // P
TB = L // P
FC = C // P
H0, D0 = 16, C // 16
PAIRS = H0 // 2
SLOT = 64
H1, D1 = 4, C // 4
HID = 4 * C
HC = HID // P
LN_EPS = 1e-6
LOG100 = float(np.log(np.float32(100.0)))
GELU_C = float(np.sqrt(2.0 / np.pi))
GELU_A = 0.044715
NEG = -1e30
RING = 3

R_QK, R_V, R_PF, R_GAM, R_SML, R_SC = 0, 512, 768, 1280, 1792, 1808
R_END = 1812



ORDER = [(name, *map(int, filter(None, rest.split(".")))) for name, _, rest in (word.partition(":") for word in """
ada split_weights0 stats0:0 norm0:0 normed0:0 split0:0 qkv0:0 root0:0 ada_rest unit0:0 hi0:0 lo0:0 turn0:0.0
stats0:1 turn0:0.1 norm0:1 stats0:2 split0:1 normed0:1 stats0:3 max0:0.0 norm0:2 qkv0:1 normed0:2 root0:1 hi0:1
split0:2 max0:0.1 max0:0.2 max0:0.3 max0:0.4 max0:0.5 unit0:1 max0:0.6 lo0:1 qkv0:2 max0:0.7 neg0:0 turn0:1.0
shift0:0 turn0:1.1 normed0:3 norm0:3 score0:0.0 root0:2 max0:1.0 score0:0.1 max0:1.1 score0:0.2 max0:1.2
max0:1.3 score0:0.3 split0:3 value0:0.0 score0:0.4 max0:1.4 value0:0.1 score0:0.5 max0:1.5 score0:0.6 take0:0.0
max0:1.6 score0:0.7 max0:1.7 hi0:2 value0:0.2 value0:0.3 unit0:2 out0:0.0 lo0:2 qkv0:3 neg0:1 take0:0.1 root0:3
turn0:2.0 shift0:1 turn0:2.1 out0:0.1 max0:2.0 score0:1.0 max0:2.1 score0:1.1 heads0:0 score0:1.2 unit0:3
max0:2.2 value0:1.0 max0:2.3 score0:1.3 max0:2.4 hi0:3 max0:2.5 lo0:3 heads0_lo:0 score0:1.4 max0:2.6
score0:1.5 take0:1.0 value0:1.1 score0:1.6 score0:1.7 max0:2.7 turn0:3.0 value0:1.2 neg0:2 shift0:2 proj0:0
turn0:3.1 score0:2.0 score0:2.1 stats1:0 take0:1.1 out0:1.0 max0:3.0 norm1:0 value0:1.3 score0:2.2 max0:3.1
out0:1.1 score0:2.3 score0:2.4 max0:3.2 max0:3.3 value0:2.0 score0:2.5 max0:3.4 value0:2.1 max0:3.5 heads0:1
max0:3.6 take0:2.0 max0:3.7 value0:2.2 neg0:3 score0:2.6 score0:2.7 split_w1 heads0_lo:1 take0:2.1 shift0:3
proj0:1 stats1:1 normed1:0 value0:2.3 out0:2.0 score0:3.0 score0:3.1 out0:2.1 heads0_lo:2 norm1:1 score0:3.2
score0:3.3 split1:0 heads0:2 value0:3.0 score0:3.4 score0:3.5 value0:3.1 take0:3.0 proj0:2 stats1:2 score0:3.6
out0:3.0 normed1:1 score0:3.7 value0:3.2 split_w2 norm1:2 fc1:0.0 split1:1 value0:3.3 take0:3.1 fc1:0.1
poly:0.0 fc1:0.2 out0:3.1 tanh:0.0 poly:0.1 heads0:3 fc1:0.3 gelu:0.0 heads0_lo:3 poly:0.2 tanh:0.1 tanh:0.2
gelu:0.1 normed1:2 split_wqkv1 fc1:1.0 proj0:3 gelu:0.2 poly:0.3 split1:2 stats1:3 poly:1.0 tanh:0.3 gelu:0.3
fc1:1.1 fc1:1.2 tanh:1.0 tanh:1.1 poly:1.1 gelu:1.0 fc1:1.3 gelu:1.1 poly:1.2 fc1:2.0 tanh:1.2 poly:1.3 norm1:3
tanh:1.3 poly:2.0 tanh:2.0 gelu:1.2 gelu:1.3 fc2:0 split1:3 stats2:0 poly:2.1 normed1:3 poly:2.2 gelu:2.0
fc1:2.1 norm2:0 fc1:2.2 fc1:2.3 tanh:2.1 tanh:2.2 gelu:2.1 fc2:1 normed2:0 fc1:3.0 tanh:2.3 poly:2.3 split2:0
fc1:3.1 tanh:3.0 gelu:2.2 gelu:2.3 poly:3.0 qkv1:0 stats2:1 fc1:3.2 gelu:3.0 root1:0 norm2:1 poly:3.1 fc1:3.3
tanh:3.1 tanh:3.2 poly:3.2 gelu:3.1 poly:3.3 gelu:3.2 normed2:1 tanh:3.3 gelu:3.3 hi1:0 split2:1 fc2:2 rope:0
stats2:2 fc2:3 qkv1:1 lo1:0 normed2:2 norm2:2 turn1:0.0 root1:1 stats2:3 turn1:0.1 split2:2 max1:0.0 max1:0.1
hi1:1 rope:1 qkv1:2 neg1:0 lo1:1 root1:2 norm2:3 turn1:1.0 turn1:1.1 shift1:0 max1:1.0 score1:0.0 score1:0.1
rope:2 max1:1.1 lo1:2 split_wout1 sum1:0 hi1:2 value1:0 normed2:3 out1:0 split2:3 turn1:2.0 neg1:1 qkv1:3
root1:3 turn1:2.1 shift1:1 max1:2.0 max1:2.1 heads1:0 neg1:2 heads1_lo:0 rope:3 score1:1.0 hi1:3 shift1:2
proj1:0 score1:1.1 lo1:3 score1:2.0 sum1:1 turn1:3.0 turn1:3.1 value1:1 max1:3.0 max1:3.1 neg1:3 score1:2.1
out1:1 shift1:3 sum1:2 heads1:1 score1:3.0 heads1_lo:1 value1:2 score1:3.1 out1:2 sum1:3 proj1:1 heads1:2
heads1_lo:2 value1:3 out1:3 proj1:2 heads1_lo:3 heads1:3 proj1:3
""".split())]
FIRST_SCORE = min(i for i, step in enumerate(ORDER) if step[0] == "max0")
AFTER_SCORES = max(i for i, step in enumerate(ORDER) if step[0] == "score0") + 1


def units_of(step):
    name, b = step[0], step[1] if len(step) > 1 else None
    i = step[2] if len(step) > 2 else None
    tiles = [TB * b + t for t in range(TB)] if b is not None else []
    if name == "ada":
        return [(("ada",), "dve")]
    if name == "ada_rest":
        return [(("ada2",), "dve"), (("flag",), "dve")] + [(("gam", c), "dve") for c in range(B)]
    if name in ("normed0", "normed1", "normed2"):
        return [(("xT", int(name[-1]), b), "act")]
    if name == "qkv0":
        return [(("qk", t), "dve") for t in tiles] + [(("v", b), "dve")]
    if name == "turn0":
        return [((w, tiles[i], u), "act") for w in ("qT", "kT") for u in range(2)]
    if name == "max0":
        return [(("mx", b, q // PAIRS, q % PAIRS), "dve") for q in (2 * i, 2 * i + 1)]
    if name == "shift0":
        return [(("shT", b), "dve")]
    if name == "out0":
        return [(("oT", b, i), "dve")]
    if name == "heads0":
        return [(("aT", b), "act")]
    if name == "proj0":
        return [(("pj", b), "dve")]
    if name == "fc1":
        return [(("f1", b, i), "act")]
    if name == "fc2":
        return [(("f2", b), "dve")]
    if name == "qkv1":
        return [(("qk1", t), "act") for t in tiles] + [(("v1", b), "act")]
    if name == "turn1":
        return [((w, tiles[i]), "act") for w in ("q1T", "k1T0", "k1T1")]
    if name == "max1":
        return [(("mx1", b, i, hp), "dve") for hp in range(2)]
    if name == "shift1":
        return [(("shT1", b), "dve")]
    if name == "out1":
        return [(("sT1", b), "dve"), (("oT1", b), "dve")]
    if name == "heads1":
        return [(("aT1", b), "act")]
    if name == "proj1":
        return [(("po", b), "dve")]
    return []


class Ring:

    def __init__(self, order):
        self.number, self.emptied = {}, {}
        counts = {"dve": 0, "act": 0}
        for step in order:
            for key, engine in units_of(step):
                assert key not in self.number, key
                self.number[key] = len(self.number)
                counts[engine] += 1
                self.emptied[key] = (engine, counts[engine])
        self.keys = list(self.number)


def positions(order, kinds):
    out = {}
    for step in order:
        if step[0] in kinds:
            out[(kinds.index(step[0]), step[1])] = len(out)
    return out


def build(nc, x, wqkv, wproj, wada, wfc1, wfc2, wnorm, wqkv1, wout1, cols, rows, rope, bias, mask, out):
    ring_plan = Ring(ORDER)
    stat_no = positions(ORDER, ["stats0", "stats1", "stats2"])
    norm_keys = [key[1:] for key in ring_plan.keys if key[0] == "xT"]
    norm_no = {key: n for n, key in enumerate(norm_keys)}

    with ExitStack() as ctx:
        def sb(name, shape, dt=F32):
            return ctx.enter_context(nc.sbuf_tensor(name, shape, dt))

        def sem(name):
            return ctx.enter_context(nc.semaphore(name))

        xs = sb("xs", [P, NT, C])
        x2 = sb("x2", [P, NT, C])
        wqkv_hi, wqkv_lo = (sb(n, [P, FC, 3 * C], F32R) for n in ("wqkv_hi", "wqkv_lo"))
        wp_hi, wp_lo = (sb(n, [P, FC, C], F32R) for n in ("wp_hi", "wp_lo"))
        wo_hi, wo_lo = (sb(n, [P, FC, C], F32R) for n in ("wo_hi", "wo_lo"))
        stage_a = sb("stage_a", [P, FC * 6 * C])
        stage_b = sb("stage_b", [P, 2048])
        gam = sb("gam", [P, B, 2 * C])
        stack = sb("stack", [P, TB, 2 * H0, SLOT], F32R)
        qstk = sb("qstk", [P, 2, PAIRS, L], F32R)
        kstk = sb("kstk", [P, 2, H0, L], F32R)
        vs = sb("vs", [P, 3, TB, H0, 32])
        ps = sb("ps", [P, 4, 2, TB, L])
        xh = sb("xh", [P, TB, C])
        xmt = sb("xmt", [P, FC, L])
        xm_hi, xm_lo = (sb(n, [P, 2, FC, L], F32R) for n in ("xm_hi", "xm_lo"))
        qk = sb("qk", [P, TB, 2 * C])
        qn = sb("qn", [P, TB, 2 * C])
        o_raw = sb("o_raw", [P, 2, 2 * L])
        o_tok = sb("o_tok", [P, TB, C])
        at_hi, at_lo = (sb(n, [P, FC, L], F32R) for n in ("at_hi", "at_lo"))
        row = sb("row", [P, R_END])
        col = sb("col", [P, 24])
        rope_sb = sb("rope_sb", [P, TB, 2, D1 // 2])
        bias_sb = sb("bias_sb", [P, TB, L])
        mask_add = sb("mask_add", [P, B, TB, L], BF16)
        ident = sb("ident", [P, P])
        ident_b = sb("ident_b", [P, P], BF16)
        ones = sb("ones", [P, 32])
        sel = sb("sel", [P, H1, P], F32R)
        silu = sb("silu", [P, 3, FC * B])
        mod = sb("mod", [P, 10, B])
        sm = sb("sm", [P, H0])
        sqs = sb("sqs", [P, 2 * H1])
        half_neg = sb("half_neg", [P, TB])
        half_pos = sb("half_pos", [P, H1])
        bnst = sb("bnst", [P, 3, B, TB, 6])
        mv = sb("mv", [P, 3, B, TB, 2])
        ve = sb("ve", [P, 3, B, TB])
        rstd = sb("rstd", [P, 3, B, TB])
        zero_col = sb("zero_col", [P, 1])
        ss = sb("ss", [P, TB, 2 * H0])
        rn = sb("rn", [P, TB, 2 * H0])
        nt = sb("nt", [P, TB, 2 * H0])
        nm = sb("nm", [P, TB, 2, PAIRS])
        shp = sb("shp", [P, TB, 2, 2 * PAIRS])
        sh1 = sb("sh1", [P, TB, 2 * H1])
        shs1 = sb("shs1", [P, L], F32R)
        rv = sb("rv", [P, 4, 4])
        nm1 = sb("nm1", [P, TB, H1])
        cnt = sb("cnt", [P, 1])
        flag = sb("flag", [1, 1], I32)

        term = stage_a[:, 2048:2048 + C]
        at = stage_a[:, 2304:2304 + FC * L].rearrange("p (f n) -> p f n", f=FC)
        shs = stage_a[0:4 * PAIRS, 2816:2816 + L]
        wnorm_sb = gam[:, 0, :].rearrange("p (f n) -> p f n", f=FC)
        mask_u8 = o_tok[:, :, :].rearrange("p t n -> p (t n)").bitcast(mybir.dt.uint8)\
            .rearrange("p (b t k) -> p b t k", b=B, t=TB)
        sel_f = o_raw[:, 1, :].rearrange("p (h n) -> p h n", h=H1)
        srep = ps[:, 0].rearrange("p a b n -> p (a b n)").rearrange("p (c n) -> p c n", n=P)
        wada_sb = stage_a[:, :].rearrange("p (f n) -> p f n", f=FC)
        rope_a = stage_a[:, 0:1024].rearrange("p (t n) -> p t n", t=2)
        rope_b = stage_a[:, 1024:2048].rearrange("p (t n) -> p t n", t=2)
        stack_flat = stack[:, :, :, :].rearrange("p t h s -> p t (h s)")
        h_hi = (qstk[:, 0], stack_flat[:, 0].rearrange("p (c n) -> p c n", c=HC))
        h_lo = (qstk[:, 1], stack_flat[:, 1].rearrange("p (c n) -> p c n", c=HC))
        w1_hi = kstk[:, 0, 0:8, :].rearrange("p a b -> p (a b)").rearrange("p (f n) -> p f n", f=FC)
        w1_lo = kstk[:, 0, 8:16, :].rearrange("p a b -> p (a b)").rearrange("p (f n) -> p f n", f=FC)
        w2_hi = kstk[:, 1, 0:8, :]
        w2_lo = kstk[:, 1, 8:16, :]
        gelu_u = ps[:, 0:2].rearrange("p c a b n -> p (c a b n)").rearrange("p (s n) -> p s n", s=4)
        gelu_z = ps[:, 2:4].rearrange("p c a b n -> p (c a b n)").rearrange("p (s n) -> p s n", s=4)
        k1 = kstk[:, 0, :, :].rearrange("p (s w h) n -> p s w h n", s=2, w=2)
        q1 = kstk[:, 1, 0:8, :].rearrange("p (s h) n -> p s h n", s=2)
        stk1 = stack_flat[:, :, 0:12 * P]\
            .rearrange("p t (g n) -> p t g n", g=12)
        v1 = vs[:, :, :, :, :].rearrange("p s t h d -> p s t (h d)")[:, :, :, 0:C]

        psx = ctx.enter_context(nc.psum_tensor("psx", [P, 2, 2, TB, L], F32))
        ring = ctx.enter_context(nc.psum_tensor("ring", [P, RING, 512], F32))
        pv = ctx.enter_context(nc.psum_tensor("pv", [P, 512], F32))

        s_col, s_row, s_bias, s_mask, s_rope, s_norm, s_wada, s_wada2, s_wq, s_wp, s_w1, s_w2, s_wq1, s_wo = (
            sem(f"in_{n}") for n in ("col", "row", "bias", "mask", "rope", "norm", "wada", "wada_rest", "wq", "wp",
                                     "w1", "w2", "wq1", "wo"))
        s_x = [sem(f"in_x{b}") for b in range(B)]
        mask_ready = sem("mask_ready")
        kzero_ready = sem("k_stack_zeros_ready")
        const_ready = sem("const_ready")
        ring_full = sem("ring_full")
        ring_dve, ring_act = sem("ring_emptied_by_vector"), sem("ring_emptied_by_scalar")
        silu_exp, silu_ready, srep_ready = sem("silu_exp"), sem("silu_ready"), sem("srep_ready")
        sml_min = sem("scale_mul_log_clamped")
        mod_ready = sem("mod_ready")
        scales_ready = sem("scales_ready")
        flag_ready = sem("flag_ready")
        w_hi, w_lo_d, w_lo_p = sem("weights_hi"), sem("weights_lo_vector"), sem("weights_lo_pool")
        xb_ready = sem("x_bias_ready")
        x2_ready, x2b_ready, x3_ready = sem("x2_ready"), sem("x2_bias_ready"), sem("x3_ready")
        stats_ready, rstd_ready = sem("stats_ready"), sem("rstd_ready")
        xh_ready, xmt_ready, xm_ready = sem("xh_ready"), sem("xmt_ready"), sem("xm_ready")
        sq_ready, seed_ready, rn_ready = sem("sq_ready"), sem("seed_ready"), sem("rn_ready")
        qn_ready, stk_hi, stk_lo = sem("qn_ready"), sem("stack_hi"), sem("stack_lo")
        stk_hi_first, stk1_hi_first = sem("stack_hi_first"), sem("stack1_hi_first")
        nm_ready, shp_ready, shift_in = sem("negmax_ready"), sem("shift_ready"), sem("shift_in")
        s_full, exp_done = sem("scores_full"), sem("exp_done")
        pv_full, pv_taken = sem("pv_full"), sem("pv_taken")
        at_ready = sem("heads_ready")
        sq1_ready, seed1_ready, rn1_ready = sem("sq1_ready"), sem("seed1_ready"), sem("rn1_ready")
        cos_done, rope_done = sem("cos_done"), sem("rope_done")
        stk1_hi, stk1_lo = sem("stack1_hi"), sem("stack1_lo")
        sh1_ready = sem("shift1_ready")
        sq_u, z_ready, t_ready, h_ready, h_hi_ready, h_lo_ready = (
            sem(n) for n in ("gelu_square", "gelu_poly", "gelu_tanh", "gelu_out", "h_hi_ready",
                             "h_lo_ready"))
        s_out = sem("out_stored")
        dve_step, pool_step = sem("vector_step"), sem("pool_step")
        block = ctx.enter_context(nc.Block())

        def full(key):
            return ring_full, ring_plan.number[key] + 1

        def emptied(key):
            engine, value = ring_plan.emptied[key]
            return (ring_dve if engine == "dve" else ring_act), value

        def bank(key):
            return ring[:, ring_plan.number[key] % RING, :]

        def previous_in_bank(key):
            n = ring_plan.number[key] - RING
            return ring_plan.keys[n] if n >= 0 else None

        def stepper(eng, s):
            count = [0]

            def step(ins):
                count[0] += 1
                ins.then_inc(s, 1)
                eng.wait_ge(s, count[0])
            return step

        def last_matmul_of_norm(kind, b):
            return [("v", b), ("f1", b, HC // 2 - 1), ("v1", b)][kind]

        norm_at = norm_keys

        @block.sync
        def _(sp):
            x_v = x.rearrange("(t p) c -> p t c", p=P)

            def load_x(b):
                sp.dma_start(xs[:, TB * b:TB * b + TB, :], x_v[:, TB * b:TB * b + TB, :])\
                  .then_inc(s_x[b], 16)

            sp.dma_start(col[:, :], cols).then_inc(s_col, 16)
            load_x(0)
            wada_v = wada.rearrange("(f p) n -> p f n", p=P)

            def load_wada(a, b_, arrived):
                sp.dma_start(wada_sb[:, :, a:b_], wada_v[:, :, a:b_]).then_inc(arrived, 16)

            load_wada(2 * C, 3 * C, s_wada)
            load_wada(4 * C, 5 * C, s_wada)
            sp.dma_start(stage_b[:, 0:FC * 3 * C].rearrange("p (f n) -> p f n", f=FC),
                         wqkv.rearrange("(f p) n -> p f n", p=P)).then_inc(s_wq, 16)
            sp.dma_start(row[:, :], rows.to_broadcast([P, R_END])).then_inc(s_row, 16)
            load_wada(3 * C, 4 * C, s_wada2)
            load_wada(5 * C, 6 * C, s_wada2)
            load_wada(0, 2 * C, s_wada2)
            sp.dma_start(wnorm_sb, wnorm.rearrange("(f p) n -> p f n", p=P)).then_inc(s_norm, 16)
            load_x(1)
            sp.dma_start(stage_b[:, FC * 3 * C:FC * 4 * C].rearrange("p (f n) -> p f n", f=FC),
                         wproj.rearrange("(f p) n -> p f n", p=P)).then_inc(s_wp, 16)
            load_x(2)
            load_x(3)
            sp.dma_start(bias_sb[:, :, :], bias.rearrange("(t p) k -> p t k", p=P)).then_inc(s_bias, 16)
            sp.dma_start(rope_sb[:, :, :, :], rope.rearrange("(t p) s d -> p t s d", p=P)).then_inc(s_rope, 16)
            sp.dma_start(mask_u8, mask.rearrange("b (t p) k -> p b t k", p=P)).then_inc(s_mask, 16)
            sp.wait_ge(*emptied(("gam", B - 1)))
            sp.wait_ge(*emptied(("ada2",)))
            sp.dma_start(stage_a[:, 0:FC * HID].rearrange("p (f n) -> p f n", f=FC),
                         wfc1.rearrange("(f p) n -> p f n", p=P)).then_inc(s_w1, 16)
            sp.wait_ge(w_hi, 2)
            sp.wait_ge(w_lo_d, 2)
            sp.dma_start(stage_b[:, :].rearrange("p (f n) -> p f n", f=HC),
                         wfc2.rearrange("(f p) n -> p f n", p=P)).then_inc(s_w2, 16)

            def shift_rows(b):
                sp.wait_ge(*emptied(("shT", b)))
                for j in range(2):
                    for par in range(2):
                        r = (2 * j + par) * PAIRS
                        sp.dma_start(qstk[SLOT * par + 48 + j:SLOT * par + 49 + j, b % 2, :, :].bitcast(F32),
                                     shs[r:r + PAIRS, :]).then_inc(shift_in, 16)

            for b in range(B):
                shift_rows(b)
            sp.wait_ge(w_hi, 3)
            sp.wait_ge(w_lo_p, 1)
            sp.dma_start(stage_a[:, 0:FC * 3 * C].rearrange("p (f n) -> p f n", f=FC),
                         wqkv1.rearrange("(f p) n -> p f n", p=P)).then_inc(s_wq1, 16)
            sp.wait_ge(w_hi, 4)
            sp.wait_ge(w_lo_p, 2)
            sp.dma_start(stage_b[:, 0:FC * C].rearrange("p (f n) -> p f n", f=FC),
                         wout1.rearrange("(f p) n -> p f n", p=P)).then_inc(s_wo, 16)
            out_v = out.rearrange("(t p) c -> p t c", p=P)
            for b in range(B):
                sp.wait_ge(*emptied(("po", b)))
                sp.dma_start(out_v[:, TB * b:TB * b + TB, :], x2[:, TB * b:TB * b + TB, :]).then_inc(s_out, 16)
            sp.wait_ge(s_out, 16 * B)

        @block.gpsimd
        def _(pool):
            g = nc.gpsimd
            step = stepper(pool, pool_step)
            g.memset(half_neg[:, :], -0.5)
            g.memset(half_pos[:, :], 0.5)
            g.memset(zero_col[:, :], 0.0)
            step(g.memset(ident[:, :], 0.0))
            step(g.affine_select(out=ident[:, :], in_=ident[:, :], compare_op=ALU.not_equal, fill=1.0, base=0,
                                 pattern=[[-1, P]], channel_multiplier=1))
            g.tensor_copy(ident_b[:, :], ident[:, :])
            g.memset(ones[:, :], 1.0).then_inc(const_ready, 1)
            step(g.memset(stack[:, :, :, 48:64].bitcast(F32), 0.0))
            g.memset(stack[:, :, H0:2 * H0, 48:50].bitcast(F32), 1.0).then_inc(const_ready, 1)
            step(g.memset(vs[:, :, :, :, 16:32], 0.0))
            g.memset(vs[:, :, :, :, 16:17], 1.0).then_inc(const_ready, 1)
            step(g.memset(sel_f, 0.0))
            g.memset(shs1[:, :].bitcast(F32), 0.0)
            for j in range(2):
                step(g.affine_select(out=sel_f, in_=sel_f, compare_op=ALU.not_equal,
                                     fill=1.0, base=-H1 * j, pattern=[[-1, H1], [0, P]],
                                     channel_multiplier=1))
            g.tensor_copy(sel[:, :, :], sel_f).then_inc(const_ready, 1)

            def rstd_of(kind, b):
                pool.wait_ge(stats_ready, stat_no[(kind, b)] + 1)
                g.tensor_tensor(rstd[:, kind, b, :], ve[:, kind, b, :], half_neg[:, 0:TB], ALU.pow)\
                 .then_inc(rstd_ready, 1)

            def inverse_root(seeded, b, n):
                pool.wait_ge(seeded, b + 1)
                y, x_, t = rn[:, :, 0:n], ss[:, :, 0:n], nt[:, :, 0:n]
                for _ in range(3):
                    step(g.tensor_tensor(t, x_, y, ALU.mult))
                    step(g.tensor_tensor(t, t, y, ALU.mult))
                    step(g.tensor_scalar(t, t, -0.5, 1.5, ALU.mult, ALU.add))
                    step(g.tensor_tensor(y, y, t, ALU.mult))

            for step_ in ORDER:
                name, b = step_[0], step_[1] if len(step_) > 1 else None
                i_ = step_[2] if len(step_) > 2 else None
                if name == "ada_rest":
                    pool.wait_ge(s_mask, 16)
                    g.tensor_scalar(mask_add[:, :, :, :], mask_u8, -1.0, -NEG, ALU.add, ALU.mult)\
                     .then_inc(mask_ready, 1)
                if name in ("stats0", "stats1", "stats2"):
                    rstd_of(int(name[-1]), b)
                if name == "qkv0":
                    for t in range(TB * b, TB * b + TB):
                        pool.wait_ge(*emptied(("qk", t)))
                        if t >= TB:
                            pool.wait_ge(stk_hi, t - TB + 1)
                            pool.wait_ge(stk_lo, t - TB + 1)
                        g.tensor_tensor(qn[:, t % TB, :], qk[:, t % TB, :], qk[:, t % TB, :], ALU.mult)\
                         .then_inc(sq_ready, 1)
                if name == "root0":
                    inverse_root(seed_ready, b, 2 * H0)
                    if b == 0:
                        pool.wait_ge(scales_ready, 1)
                    g.tensor_tensor(rn[:, :, 0:H0], rn[:, :, 0:H0], sm[:, :].unsqueeze(1).to_broadcast([P, TB, H0]),
                                    ALU.mult).then_inc(rn_ready, 1)
                if name == "heads0":
                    tiles = slice(TB * b, TB * b + TB)
                    pool.wait_ge(*emptied(("gam", b)))
                    pool.wait_ge(xh_ready, norm_no[(0, b)] + 1)
                    if b >= 1:
                        pool.wait_ge(x2b_ready, b)
                    step(g.tensor_tensor(term, gam[:, b, 0:C], row[:, R_PF:R_PF + C], ALU.mult))
                    g.tensor_tensor(xs[:, tiles, :], xs[:, tiles, :], term.unsqueeze(1).to_broadcast([P, TB, C]),
                                    ALU.add).then_inc(xb_ready, 1)
                if name == "stats1":
                    tiles = slice(TB * b, TB * b + TB)
                    pool.wait_ge(xb_ready, b + 1)
                    step(g.tensor_tensor(term, gam[:, b, C:2 * C], row[:, R_PF + C:R_PF + 2 * C], ALU.mult))
                    pool.wait_ge(x2_ready, b + 1)
                    g.tensor_tensor(xs[:, tiles, :], x2[:, tiles, :], term.unsqueeze(1).to_broadcast([P, TB, C]),
                                    ALU.add).then_inc(x2b_ready, 1)
                if name == "split_w1":
                    pool.wait_ge(w_hi, 3)
                    g.tensor_tensor(w1_lo, stage_a[:, 0:FC * HID].rearrange("p (f n) -> p f n", f=FC),
                                    w1_hi, ALU.subtract).then_inc(w_lo_p, 1)
                if name == "split_w2":
                    pool.wait_ge(w_hi, 4)
                    g.tensor_tensor(w2_lo, stage_b[:, :].rearrange("p (f n) -> p f n", f=HC),
                                    w2_hi, ALU.subtract).then_inc(w_lo_p, 1)
                if name == "split_wqkv1":
                    pool.wait_ge(w_hi, 5)
                    g.tensor_tensor(wqkv_lo[:, :, :], stage_a[:, 0:FC * 3 * C].rearrange("p (f n) -> p f n", f=FC),
                                    wqkv_hi[:, :, :], ALU.subtract).then_inc(w_lo_p, 1)
                if name == "split_wout1":
                    pool.wait_ge(w_hi, 6)
                    g.tensor_tensor(wo_lo[:, :, :], stage_b[:, 0:FC * C].rearrange("p (f n) -> p f n", f=FC),
                                    wo_hi[:, :, :], ALU.subtract).then_inc(w_lo_p, 1)
                if name == "gelu":
                    n = (HC // 2) * b + i_
                    pool.wait_ge(h_hi_ready, n + 1)
                    g.tensor_tensor(h_lo[b % 2][:, 2 * i_:2 * i_ + 2, :],
                                    gelu_u[:, n % 4, :].rearrange("p (a n) -> p a n", a=2),
                                    h_hi[b % 2][:, 2 * i_:2 * i_ + 2, :], ALU.subtract).then_inc(h_lo_ready, 1)
                if name == "qkv1":
                    for t in range(TB * b, TB * b + TB):
                        pool.wait_ge(*emptied(("qk1", t)))
                        if t >= TB:
                            pool.wait_ge(stk1_hi, t - TB + 1)
                            pool.wait_ge(stk1_lo, t - TB + 1)
                        g.tensor_tensor(qn[:, t % TB, :], qk[:, t % TB, :], qk[:, t % TB, :], ALU.mult)\
                         .then_inc(sq1_ready, 1)
                if name == "root1":
                    inverse_root(seed1_ready, b, 2 * H1)
                    g.tensor_tensor(rn[:, :, 0:2 * H1], rn[:, :, 0:2 * H1],
                                    sqs[:, :].unsqueeze(1).to_broadcast([P, TB, 2 * H1]), ALU.mult).then_inc(rn1_ready, 1)
                if name == "rope":
                    for t in range(TB * b, TB * b + TB):
                        if t == 0:
                            pool.wait_ge(s_rope, 16)
                            pool.wait_ge(w_hi, 5)
                            pool.wait_ge(w_lo_p, 3)
                        if t >= TB:
                            pool.wait_ge(rope_done, t - TB + 1)
                        g.tensor_tensor(rope_a[:, t % 2, :].rearrange("p (g d) -> p g d", d=D1 // 2),
                                        qk[:, t % TB, :].rearrange("p (g d) -> p g d", d=D1 // 2),
                                        rope_sb[:, t % TB, 0:1, :].to_broadcast([P, 4 * H1, D1 // 2]),
                                        ALU.mult).then_inc(cos_done, 1)
                if name == "ada":
                    pool.wait_ge(s_row, 16)
                    g.tensor_tensor(sqs[:, 0:H1], row[:, R_SC:R_SC + H1], half_pos[:, 0:H1], ALU.pow)
                    step(g.tensor_tensor(sqs[:, H1:2 * H1], row[:, R_SC:R_SC + H1], half_pos[:, 0:H1], ALU.pow))

        @block.scalar
        def _(act):
            a = nc.scalar

            def split_hi(s, amount, dst, src):
                act.wait_ge(s, amount)
                a.activation(dst, src, ACT.Copy).then_inc(w_hi, 1)

            def modulate(kind, b):
                key = ("xT", kind, b)
                n = norm_no[(kind, b)]
                act.wait_ge(*full(key))
                if n == 0:
                    act.wait_ge(mod_ready, 1)
                if kind == 1 and b == 0:
                    act.wait_ge(mod_ready, 2)
                if n >= 1:
                    act.wait_ge(xm_ready, n)
                src = bank(key).rearrange("p (f n) -> p f n", f=FC)
                for f in range(FC):
                    if kind == 2:
                        ins = a.activation(xmt[:, f, :], src[:, f, :], ACT.Identity, bias=0.0,
                                           scale=mod[:, 8 + f, b:b + 1])
                    else:
                        ins = a.activation(xmt[:, f, :], src[:, f, :], ACT.Identity,
                                           bias=mod[:, 4 + 2 * kind + f, b:b + 1],
                                           scale=mod[:, 2 * kind + f, b:b + 1])
                ins.then_inc(ring_act, 1)

            def exps(n, free):
                act.wait_ge(s_full, n + 1)
                if n == 0:
                    act.wait_ge(*emptied(("gam", B - 1)))
                if free:
                    act.wait_ge(pv_full, free)
                a.activation(ps[:, n % 4], psx[:, n % 2], ACT.Exp).then_inc(exp_done, 1)

            def take_heads(key, read_before):
                act.wait_ge(*full(key))
                if read_before is not None:
                    act.wait_ge(*full(read_before))
                src = bank(key).rearrange("p (f n) -> p f n", f=FC)
                a.activation(at[:, :, :], src, ACT.Copy)
                a.activation(at_hi[:, :, :], src, ACT.Copy).then_inc(ring_act, 1)

            def take_o(b, u):
                k = 2 * b + u
                act.wait_ge(pv_full, 4 * b + 2 * u + 2)
                if k >= 2:
                    act.wait_ge(*full(("oT", (k - 2) // 2, k % 2)))
                else:
                    act.wait_ge(const_ready, 4)
                    act.wait_ge(flag_ready, 1)
                a.activation(o_raw[:, k % 2, :], pv[:, :], ACT.Copy).then_inc(pv_taken, 1)

            for step_ in ORDER:
                name, b = step_[0], step_[1] if len(step_) > 1 else None
                i_ = step_[2] if len(step_) > 2 else None
                if name == "ada":
                    act.wait_ge(s_col, 16)
                    a.activation(silu[:, 0, :], col[:, 0:FC * B], ACT.Exp, scale=-1.0).then_inc(silu_exp, 1)
                    act.wait_ge(sml_min, 1)
                    a.activation(sm[:, :], sm[:, :], ACT.Exp).then_inc(scales_ready, 1)
                if name == "split_weights0":
                    split_hi(s_wq, 16, wqkv_hi[:, :, :], stage_b[:, 0:FC * 3 * C].rearrange("p (f n) -> p f n", f=FC))
                    split_hi(s_wp, 16, wp_hi[:, :, :], stage_b[:, FC * 3 * C:FC * 4 * C].rearrange("p (f n) -> p f n", f=FC))
                if name in ("normed0", "normed1", "normed2"):
                    modulate(int(name[-1]), b)
                if name == "hi0":
                    for t in range(TB * b, TB * b + TB):
                        act.wait_ge(qn_ready, t + 1)
                        if t >= TB:
                            act.wait_ge(*full(("kT", t - TB, 1)))
                        s = stack[:, t % TB]
                        q = qn[:, t % TB, :].rearrange("p (h d) -> p h d", d=D0)
                        a.activation(s[:, :, 0:16], q, ACT.Copy).then_inc(stk_hi_first, 1)
                        a.activation(s[:, 0:H0, 16:32], q[:, 0:H0], ACT.Copy)
                        a.activation(s[:, H0:2 * H0, 32:48], q[:, H0:2 * H0], ACT.Copy).then_inc(stk_hi, 1)
                if name == "turn0":
                    t = TB * b + i_
                    tok = slice(i_ * P, i_ * P + P)
                    if t == 0:
                        act.wait_ge(kzero_ready, 1)
                    if i_ == 0 and b >= 2:
                        act.wait_ge(s_full, PAIRS * (b - 1))
                    for u in range(2):
                        key = ("qT", t, u)
                        act.wait_ge(*full(key))
                        a.activation(qstk[:, b % 2, 4 * u:4 * u + 4, tok],
                                     bank(key).rearrange("p (a n) -> p a n", a=4), ACT.Copy).then_inc(ring_act, 1)
                    for u in range(2):
                        key = ("kT", t, u)
                        act.wait_ge(*full(key))
                        src = bank(key).rearrange("p (a n) -> p a n", a=4)
                        dst = kstk[:, b % 2, :, tok].rearrange("p (a c) n -> p a c n", c=2)[:, 4 * u:4 * u + 4]
                        a.activation(dst[0:SLOT, :, 0, :], src[0:SLOT], ACT.Copy)
                        a.activation(dst[SLOT:P, :, 1, :], src[SLOT:P], ACT.Copy).then_inc(ring_act, 1)
                if name == "score0":
                    n = PAIRS * b + i_
                    exps(n, (n - 4) // 2 + 1 if n >= 4 else 0)
                if name == "take0":
                    take_o(b, i_)
                if name == "heads0":
                    take_heads(("aT", b), ("pj", b - 1) if b >= 1 else None)
                if name == "split_w1":
                    act.wait_ge(s_full, 3 * PAIRS)
                    split_hi(s_w1, 16, w1_hi, stage_a[:, 0:FC * HID].rearrange("p (f n) -> p f n", f=FC))
                if name == "split_w2":
                    act.wait_ge(s_full, 4 * PAIRS)
                    split_hi(s_w2, 16, w2_hi, stage_b[:, :].rearrange("p (f n) -> p f n", f=HC))
                if name == "split_wqkv1":
                    act.wait_ge(*full(("v", B - 1)))
                    split_hi(s_wq1, 16, wqkv_hi[:, :, :], stage_a[:, 0:FC * 3 * C].rearrange("p (f n) -> p f n", f=FC))
                if name == "split_wout1":
                    split_hi(s_wo, 16, wo_hi[:, :, :], stage_b[:, 0:FC * C].rearrange("p (f n) -> p f n", f=FC))
                if name == "fc1":
                    n = (HC // 2) * b + i_
                    key = ("f1", b, i_)
                    if n == 0:
                        act.wait_ge(pv_full, 4 * B)
                    act.wait_ge(*full(key))
                    if n >= 4:
                        act.wait_ge(h_lo_ready, n - 3)
                    for i in range(2):
                        last = a.activation(gelu_u[:, n % 4, i * L:(i + 1) * L], bank(key)[:, i * L:(i + 1) * L],
                                            ACT.Identity, bias=col[:, 16 + 2 * i_ + i:17 + 2 * i_ + i])
                    last.then_inc(ring_act, 1)
                    act.wait_ge(*emptied(key))
                    a.activation(gelu_z[:, n % 4, :], gelu_u[:, n % 4, :], ACT.Square).then_inc(sq_u, 1)
                if name == "tanh":
                    n = (HC // 2) * b + i_
                    act.wait_ge(z_ready, n + 1)
                    a.activation(gelu_z[:, n % 4, :], gelu_z[:, n % 4, :], ACT.Tanh, scale=GELU_C * GELU_A)\
                     .then_inc(t_ready, 1)
                if name == "qkv1":
                    for t in range(TB * b, TB * b + TB):
                        act.wait_ge(*full(("qk1", t)))
                        if t < TB:
                            act.wait_ge(qn_ready, NT)
                        else:
                            act.wait_ge(cos_done, t - TB + 1)
                            act.wait_ge(rope_done, t - TB + 1)
                        a.activation(qk[:, t % TB, :], bank(("qk1", t)), ACT.Copy).then_inc(ring_act, 1)
                    act.wait_ge(*full(("v1", b)))
                    if b >= 3:
                        act.wait_ge(pv_full, 16 + 2 * (b - 3) + 2)
                    a.activation(v1[:, b % 3, :, :], bank(("v1", b)).rearrange("p (t n) -> p t n", t=TB), ACT.Copy)\
                     .then_inc(ring_act, 1)
                if name == "hi1":
                    for t in range(TB * b, TB * b + TB):
                        act.wait_ge(rope_done, t + 1)
                        act.wait_ge(*full(("k1T1", t - TB) if t >= TB else ("f2", B - 1)))
                        s = stk1[:, t % TB]
                        r = qn[:, t % TB, :].rearrange("p (h d) -> p h d", d=D1)
                        a.activation(s[:, 0:H1, 0:D1], r[:, 0:H1], ACT.Copy)
                        a.activation(s[:, H1:2 * H1, 0:D1], r[:, H1:2 * H1], ACT.Copy).then_inc(stk1_hi_first, 1)
                        a.activation(s[:, H1:2 * H1, D1:2 * D1], r[:, H1:2 * H1], ACT.Copy).then_inc(stk1_hi, 1)
                if name == "turn1":
                    t = TB * b + i_
                    tok = slice(i_ * P, i_ * P + P)
                    if i_ == 0:
                        act.wait_ge(*full(("f2", B - 1)))
                        if b >= 2:
                            act.wait_ge(s_full, PAIRS * B + 2 * (b - 1))
                    for i, w in enumerate(("q1T", "k1T0", "k1T1")):
                        act.wait_ge(*full((w, t)))
                        dst = q1[:, b % 2, :, tok] if i == 0 else k1[:, b % 2, i - 1, :, tok]
                        a.activation(dst, bank((w, t)).rearrange("p (a n) -> p a n", a=4), ACT.Copy)\
                         .then_inc(ring_act, 1)
                if name == "score1":
                    n = PAIRS * B + 2 * b + i_
                    if n == PAIRS * B:
                        act.wait_ge(h_lo_ready, B * HC // 2)
                    exps(n, 4 * B + 2 * (b - 2) + 2 if b >= 2 else 4 * B)
                if name == "sum1":
                    act.wait_ge(pv_full, 16 + 2 * b + 1)
                    if b == 0:
                        act.wait_ge(*full(("oT", B - 1, 1)))
                    else:
                        act.wait_ge(*full(("sT1", b - 1)))
                    a.activation(o_raw[:, 0, 0:L], pv[:, 0:L], ACT.Copy).then_inc(pv_taken, 1)
                if name == "value1":
                    act.wait_ge(pv_full, 16 + 2 * b + 2)
                    if b >= 1:
                        act.wait_ge(*full(("oT1", b - 1)))
                    a.activation(o_raw[:, 1, :], pv[:, :], ACT.Copy).then_inc(pv_taken, 1)
                if name == "heads1":
                    take_heads(("aT1", b), ("pj", B - 1) if b == 0 else ("po", b - 1))

        @block.tensor
        def _(pe):
            mm = nc.tensor.matmul

            def claim(key):
                before = previous_in_bank(key)
                if before is not None:
                    pe.wait_ge(*emptied(before))
                return bank(key)

            def three(dst, lhs, rhs, start, stop):
                mm(dst, lhs[0], rhs[0], start=start, stop=False)
                mm(dst, lhs[0], rhs[1], start=False, stop=False)
                return mm(dst, lhs[1], rhs[0], start=False, stop=stop)

            def transposes(dst, sources, idt=None):
                for i, src in enumerate(sources):
                    last = nc.tensor.transpose(dst[:, i * P:(i + 1) * P], src, ident[:, :])
                return last

            def adaptive(dst, chunks):
                for j in chunks:
                    for f in range(FC):
                        last = mm(dst[:, B * j:B * j + B], wada_sb[:, f, 2 * C + j * P:2 * C + (j + 1) * P],
                                  silu[:, 2, f * B:(f + 1) * B], start=(f == 0), stop=(f == FC - 1))
                return last

            def norm_transposed(kind, b):
                key = ("xT", kind, b)
                dst = claim(key)
                pe.wait_ge(xh_ready, norm_no[(kind, b)] + 1)
                transposes(dst, [xh[:, t, f * P:(f + 1) * P] for f in range(FC) for t in range(TB)])\
                    .then_inc(ring_full, 1)

            def operand(kind, b, f, tok):
                s = norm_no[(kind, b)] % 2
                return xm_hi[:, s, f, tok], xm_lo[:, s, f, tok]

            def qkv_products(kind, b, wqk, names):
                pe.wait_ge(xm_ready, norm_no[(kind, b)] + 1)
                for i in range(TB):
                    key = (names[0], TB * b + i)
                    dst = claim(key)
                    tok = slice(i * P, i * P + P)
                    for f in range(FC):
                        last = three(dst, operand(kind, b, f, tok), (wqk[0][:, f, 0:2 * C], wqk[1][:, f, 0:2 * C]),
                                     f == 0, f == FC - 1)
                    last.then_inc(ring_full, 1)
                key = (names[1], b)
                dst = claim(key)
                for i in range(TB):
                    tok = slice(i * P, i * P + P)
                    for f in range(FC):
                        last = three(dst[:, i * C:(i + 1) * C], operand(kind, b, f, tok),
                                     (wqk[0][:, f, 2 * C:3 * C], wqk[1][:, f, 2 * C:3 * C]), f == 0, f == FC - 1)
                last.then_inc(ring_full, 1)

            def max_scores(b, qc, p, with_bias):
                key = ("mx", b, qc, p)
                dst = claim(key)
                if (qc, p) == (0, 0):
                    pe.wait_ge(*emptied(("kT", TB * b + 1, 1)))
                last = mm(dst, qstk[:, b % 2, p, qc * P:(qc + 1) * P], kstk[:, b % 2, 2 * p:2 * p + 2, :],
                          start=True, stop=not with_bias)
                if with_bias:
                    for i in range(2):
                        last = mm(dst[:, i * L:(i + 1) * L], ident[:, :], bias_sb[:, qc, :], start=False, stop=(i == 1))
                last.then_inc(ring_full, 1)

            def shift_transposed(b):
                dst = claim(("shT", b))
                pe.wait_ge(shp_ready, b + 1)
                for qc in range(TB):
                    last = nc.tensor.transpose(dst[0:4 * PAIRS, qc * P:(qc + 1) * P],
                                               shp[:, qc, :, :].rearrange("p j h -> p (j h)"), ident[:, :])
                last.then_inc(ring_full, 1)

            def key_major_scores(b, p, with_bias):
                n = PAIRS * b + p
                if n >= 2:
                    pe.wait_ge(exp_done, n - 1)
                if p == 0:
                    pe.wait_ge(shift_in, 64 * (b + 1))
                dst = psx[:, n % 2]
                for i in range(2):
                    for kc in range(TB):
                        keys = slice(kc * P, kc * P + P)
                        last = mm(dst[:, i, kc, :], kstk[:, b % 2, 2 * p + i, keys], qstk[:, b % 2, p, :],
                                  start=True, stop=not with_bias)
                        if with_bias:
                            for qc in range(TB):
                                last = mm(dst[:, i, kc, qc * P:(qc + 1) * P], bias_sb[:, qc, keys], ident[:, :],
                                          start=False, stop=(qc == TB - 1))
                last.then_inc(s_full, 1)

            def weighted_values(b, g):
                if g % 2 == 0 and (b or g):
                    pe.wait_ge(pv_taken, 2 * b + g // 2)
                pe.wait_ge(exp_done, PAIRS * b + 2 * g + 2)
                if g == 0:
                    pe.wait_ge(*emptied(("v", b)))
                    pe.wait_ge(const_ready, 3)
                cols_ = slice((g % 2) * L, (g % 2) * L + L)
                for kc in range(TB):
                    for i in range(4):
                        slot = (PAIRS * b + 2 * g + i // 2) % 4
                        last = mm(pv[32 * i:32 * i + 32, cols_], vs[:, b % 3, kc, 4 * g + i, :],
                                  ps[:, slot, i % 2, kc, :], start=(kc == 0), stop=(kc == TB - 1))
                last.then_inc(pv_full, 1)

            def output_token_major(b, u):
                key = ("oT", b, u)
                dst = claim(key)
                pe.wait_ge(pv_taken, 2 * b + u + 1)
                k = 2 * b + u
                transposes(dst, [o_raw[:, k % 2, i * P:(i + 1) * P] for i in range(4)]).then_inc(ring_full, 1)

            def heads_transposed(b, key, source):
                dst = claim(key)
                pe.wait_ge(*emptied(source))
                transposes(dst, [o_tok[:, t, f * P:(f + 1) * P] for f in range(FC) for t in range(TB)])\
                    .then_inc(ring_full, 1)

            def project(key, n, w):
                dst = claim(key)
                pe.wait_ge(at_ready, n + 1)
                for i in range(TB):
                    tok = slice(i * P, i * P + P)
                    for f in range(FC):
                        last = three(dst[:, i * C:(i + 1) * C], (at_hi[:, f, tok], at_lo[:, f, tok]),
                                     (w[0][:, f, :], w[1][:, f, :]), f == 0, f == FC - 1)
                last.then_inc(ring_full, 1)

            def walk(steps, with_bias):
                for step_ in steps:
                    name, b = step_[0], step_[1] if len(step_) > 1 else None
                    i_ = step_[2] if len(step_) > 2 else None
                    if name == "ada":
                        pe.wait_ge(const_ready, 1)
                        pe.wait_ge(s_wada, 32)
                        pe.wait_ge(silu_ready, 1)
                        adaptive(claim(("ada",)), (0, 1, 4, 5)).then_inc(ring_full, 1)
                    if name == "ada_rest":
                        pe.wait_ge(s_wada2, 48)
                        pe.wait_ge(s_norm, 16)
                        dst = claim(("ada2",))
                        adaptive(dst, (2, 3, 6, 7))
                        for j in range(FC):
                            for f in range(FC):
                                last = mm(dst[:, B * (8 + j):B * (9 + j)], wnorm_sb[:, f, j * P:(j + 1) * P],
                                          col[:, f * B:(f + 1) * B], start=(f == 0), stop=(f == FC - 1))
                        last.then_inc(ring_full, 1)
                        dst = claim(("flag",))
                        pe.wait_ge(flag_ready, 1)
                        mm(dst[0:1, 0:1], cnt[:, :], ones[:, 0:1], start=True, stop=True).then_inc(ring_full, 1)
                        pe.wait_ge(srep_ready, 1)
                        for i in range(B):
                            dst = claim(("gam", i))
                            for f in range(FC):
                                last = mm(dst, srep[:, f * B + i, :], wada_sb[:, f, 0:2 * C], start=(f == 0),
                                          stop=(f == FC - 1))
                            last.then_inc(ring_full, 1)
                    if name in ("normed0", "normed1", "normed2"):
                        norm_transposed(int(name[-1]), b)
                    if name == "qkv0":
                        if b == 0:
                            pe.wait_ge(w_lo_d, 1)
                        qkv_products(0, b, (wqkv_hi, wqkv_lo), ("qk", "v"))
                    if name == "turn0":
                        t = TB * b + i_
                        if t == 0:
                            pe.wait_ge(const_ready, 2)
                        pe.wait_ge(stk_hi, t + 1)
                        pe.wait_ge(stk_lo, t + 1)
                        flat = stack_flat[:, t % TB].bitcast(F32)
                        for w, base in (("qT", 0), ("kT", H0 * SLOT)):
                            for u in range(2):
                                dst = claim((w, t, u))
                                transposes(dst, [flat[:, base + (4 * u + i) * P:base + (4 * u + i + 1) * P]
                                                 for i in range(4)]).then_inc(ring_full, 1)
                    if name == "max0":
                        for q in (2 * i_, 2 * i_ + 1):
                            max_scores(b, q // PAIRS, q % PAIRS, with_bias)
                    if name == "shift0":
                        shift_transposed(b)
                    if name == "score0":
                        key_major_scores(b, i_, with_bias)
                    if name == "value0":
                        weighted_values(b, i_)
                    if name == "out0":
                        output_token_major(b, i_)
                    if name == "heads0":
                        heads_transposed(b, ("aT", b), ("oT", b, 1))
                    if name == "proj0":
                        if b == 0:
                            pe.wait_ge(w_lo_d, 2)
                        project(("pj", b), b, (wp_hi, wp_lo))
                    if name == "fc1":
                        if i_ == 0:
                            pe.wait_ge(xm_ready, norm_no[(1, b)] + 1)
                        if b == 0 and i_ == 0:
                            pe.wait_ge(w_lo_p, 1)
                        dst = claim(("f1", b, i_))
                        for i in range(2):
                            c = slice((2 * i_ + i) * P, (2 * i_ + i + 1) * P)
                            for f in range(FC):
                                last = three(dst[:, i * L:(i + 1) * L], (w1_hi[:, f, c], w1_lo[:, f, c]),
                                             operand(1, b, f, slice(0, L)), f == 0, f == FC - 1)
                        last.then_inc(ring_full, 1)
                    if name == "fc2":
                        if b == 0:
                            pe.wait_ge(w_lo_p, 2)
                        dst = claim(("f2", b))
                        pe.wait_ge(h_lo_ready, (HC // 2) * (b + 1))
                        for i in range(TB):
                            tok = slice(i * P, i * P + P)
                            for c in range(HC):
                                last = three(dst[:, i * C:(i + 1) * C], (h_hi[b % 2][:, c, tok], h_lo[b % 2][:, c, tok]),
                                             (w2_hi[:, c, :], w2_lo[:, c, :]), c == 0, c == HC - 1)
                        last.then_inc(ring_full, 1)
                    if name == "qkv1":
                        if b == 0:
                            pe.wait_ge(w_lo_p, 3)
                        qkv_products(2, b, (wqkv_hi, wqkv_lo), ("qk1", "v1"))
                    if name == "turn1":
                        t = TB * b + i_
                        pe.wait_ge(stk1_hi, t + 1)
                        pe.wait_ge(stk1_lo, t + 1)
                        for i, w in enumerate(("q1T", "k1T0", "k1T1")):
                            dst = claim((w, t))
                            transposes(dst, [stk1[:, t % TB, 4 * i + h, :].bitcast(F32) for h in range(H1)])\
                                .then_inc(ring_full, 1)
                    if name == "max1":
                        for hp in range(2):
                            dst = claim(("mx1", b, i_, hp))
                            if (i_, hp) == (0, 0):
                                pe.wait_ge(*emptied(("k1T1", TB * b + 1)))
                            for i in range(2):
                                h = 2 * hp + i
                                for w in range(2):
                                    mm(dst[:, i * L:(i + 1) * L], q1[:, b % 2, h, i_ * P:(i_ + 1) * P],
                                       k1[:, b % 2, w, h, :], start=(w == 0), stop=False)
                                last = mm(dst[:, i * L:(i + 1) * L], ident_b[:, :], mask_add[:, b, i_, :],
                                          start=False, stop=True)
                            last.then_inc(ring_full, 1)
                    if name == "shift1":
                        dst = claim(("shT1", b))
                        pe.wait_ge(sh1_ready, b + 1)
                        for qc in range(TB):
                            last = nc.tensor.transpose(dst[0:2 * H1, qc * P:(qc + 1) * P], sh1[:, qc, :], ident[:, :])
                        last.then_inc(ring_full, 1)
                    if name == "score1":
                        n = PAIRS * B + 2 * b + i_
                        pe.wait_ge(exp_done, n - 1)
                        if i_ == 0:
                            pe.wait_ge(*emptied(("shT1", b)))
                            pe.wait_ge(const_ready, 4)
                        for i in range(2):
                            h = 2 * i_ + i
                            for kc in range(TB):
                                keys = slice(kc * P, kc * P + P)
                                dst = psx[:, n % 2, i, kc, :]
                                for w in range(2):
                                    mm(dst, k1[:, b % 2, w, h, keys], q1[:, b % 2, h, :],
                                       start=(w == 0), stop=False)
                                for qc in range(TB):
                                    mm(dst[:, qc * P:(qc + 1) * P], mask_add[:, b, qc, keys], ident_b[:, :],
                                       start=False, stop=False)
                                last = mm(dst, sel[:, h, :], shs1[:, :], start=False, stop=True)
                        last.then_inc(s_full, 1)
                    if name == "sum1":
                        first = PAIRS * B + 2 * b
                        pe.wait_ge(pv_taken, 2 * B + 2 * b)
                        pe.wait_ge(exp_done, first + 2)
                        for kc in range(TB):
                            for h in range(H1):
                                last = mm(pv[32 * h:32 * h + 32, 0:L], ones[:, :], ps[:, (first + h // 2) % 4, h % 2, kc, :],
                                          start=(kc == 0), stop=(kc == TB - 1))
                        last.then_inc(pv_full, 1)
                    if name == "value1":
                        first = PAIRS * B + 2 * b
                        pe.wait_ge(pv_taken, 2 * B + 2 * b + 1)
                        for hp in range(2):
                            for kc in range(TB):
                                for i in range(2):
                                    h = 2 * hp + i
                                    last = mm(pv[64 * i:64 * i + 64, hp * L:(hp + 1) * L],
                                              v1[:, b % 3, kc, h * D1:(h + 1) * D1],
                                              ps[:, (first + hp) % 4, i, kc, :], start=(kc == 0), stop=(kc == TB - 1))
                        last.then_inc(pv_full, 1)
                    if name == "out1":
                        dst = claim(("sT1", b))
                        transposes(dst, [o_raw[:, 0, qc * P:(qc + 1) * P] for qc in range(TB)]).then_inc(ring_full, 1)
                        dst = claim(("oT1", b))
                        pe.wait_ge(pv_taken, 2 * B + 2 * b + 2)
                        transposes(dst, [o_raw[:, 1, i * P:(i + 1) * P] for i in range(4)]).then_inc(ring_full, 1)
                    if name == "heads1":
                        heads_transposed(b, ("aT1", b), ("oT1", b))
                    if name == "proj1":
                        if b == 0:
                            pe.wait_ge(w_lo_p, 4)
                        project(("po", b), B + b, (wo_hi, wo_lo))

            walk(ORDER[:FIRST_SCORE], False)
            pe.wait_ge(*emptied(("flag",)))
            bias_flag = nc.tensor.value_load(flag[0:1, 0:1], min_val=0, max_val=1 << 20)
            with nc.tensor.If(bias_flag == 0):
                walk(ORDER[FIRST_SCORE:AFTER_SCORES], False)
            with nc.tensor.If(bias_flag != 0):
                walk(ORDER[FIRST_SCORE:AFTER_SCORES], True)
            walk(ORDER[AFTER_SCORES:], False)

        @block.vector
        def _(dve):
            v = nc.vector
            step = stepper(dve, dve_step)

            def adaptive(key, firsts, with_norm):
                dve.wait_ge(*full(key))
                src = bank(key)[:, 0:10 * B].rearrange("p (j n) -> p j n", n=B)
                for j in firsts:
                    last = v.tensor_tensor(mod[:, j:j + 2, :], src[:, j:j + 2, :],
                                           col[:, 8 + j:10 + j].unsqueeze(2).to_broadcast([P, 2, B]), ALU.add)
                    if j < 4:
                        step(last)
                if with_norm:
                    last = v.tensor_scalar(mod[:, 8:10, :], src[:, 8:10, :], 1.0, None, ALU.add)
                last.then_inc(ring_dve, 1)
                dve.wait_ge(*emptied(key))
                v.tensor_scalar(mod[:, firsts[0]:firsts[0] + 2, :], mod[:, firsts[0]:firsts[0] + 2, :], 1.0, None,
                                ALU.add).then_inc(mod_ready, 1)

            def seed(b, n, least, seeded):
                y, x_, t = rn[:, :, 0:n], ss[:, :, 0:n], nt[:, :, 0:n]
                step(least)
                step(v.tensor_scalar(t.bitcast(I32), x_.bitcast(I32), 1, None, ALU.logical_shift_right))
                v.tensor_scalar(y.bitcast(I32), t.bitcast(I32), -1.0, float(0x5f3759df), ALU.mult, ALU.add)\
                 .then_inc(seeded, 1)

            def statistics(kind, b, src):
                for i in range(TB):
                    step(v.bn_stats(bnst[:, kind, b, i, :], src[:, TB * b + i, :]))
                for i in range(TB):
                    step(v.bn_aggr(mv[:, kind, b, i, :], bnst[:, kind, b, i, :]))
                if kind < 2:
                    v.tensor_scalar(ve[:, kind, b, :], mv[:, kind, b, :, 1], LN_EPS, None, ALU.add).then_inc(stats_ready, 1)
                else:
                    step(v.tensor_tensor(ve[:, kind, b, :], mv[:, kind, b, :, 0], mv[:, kind, b, :, 0], ALU.mult))
                    v.scalar_tensor_tensor(ve[:, kind, b, :], ve[:, kind, b, :], LN_EPS, mv[:, kind, b, :, 1],
                                           ALU.add, ALU.add).then_inc(stats_ready, 1)

            def normalise(kind, b, src):
                n = norm_no[(kind, b)]
                dve.wait_ge(rstd_ready, stat_no[(kind, b)] + 1)
                if n >= 1:
                    dve.wait_ge(*full(("xT",) + norm_at[n - 1]))
                for i in range(TB):
                    mean = mv[:, kind, b, i, 0:1] if kind < 2 else zero_col[:, :]
                    ins = v.tensor_scalar(xh[:, i, :], src[:, TB * b + i, :], mean, rstd[:, kind, b, i:i + 1],
                                          ALU.subtract, ALU.mult)
                ins.then_inc(xh_ready, 1)

            def split_norm(kind, b):
                n = norm_no[(kind, b)]
                dve.wait_ge(*emptied(("xT", kind, b)))
                if n >= 2:
                    dve.wait_ge(*full(last_matmul_of_norm(*norm_at[n - 2])))
                step(v.tensor_copy(xm_hi[:, n % 2], xmt[:, :, :]))
                v.tensor_tensor(xm_lo[:, n % 2], xmt[:, :, :], xm_hi[:, n % 2], ALU.subtract).then_inc(xm_ready, 1)

            def row_max(b, qc, p):
                key = ("mx", b, qc, p)
                dve.wait_ge(*full(key))
                v.tensor_reduce(nm[:, qc, :, p], bank(key).rearrange("p (h n) -> p h n", h=2), AX.X, ALU.max,
                                negate=True).then_inc(ring_dve, 1)

            def token_major_output(b, u):
                key = ("oT", b, u)
                dve.wait_ge(*full(key))
                src = bank(key).rearrange("p (q i s) -> p q i s", q=4, i=4)
                if 2 * b + u >= 1:
                    dve.wait_ge(*emptied(("oT", (2 * b + u - 1) // 2, (u + 1) % 2)))
                step(v.reciprocal(rv[:, :, :], src[:, :, :, D0]))
                if u == 0 and b == 0:
                    dve.wait_ge(mask_ready, 1)
                if u == 0 and b >= 1:
                    dve.wait_ge(*full(("aT", b - 1)))
                ot = o_tok[:, :, :].rearrange("p t (h d) -> p t h d", d=D0)
                for half in range(2):
                    h = 8 * u + 4 * half
                    ins = v.tensor_tensor(ot[:, :, h:h + 4, :], src[:, 2 * half:2 * half + 2, :, 0:D0],
                                          rv[:, 2 * half:2 * half + 2, :].unsqueeze(3).to_broadcast([P, TB, 4, D0]),
                                          ALU.mult)
                ins.then_inc(ring_dve, 1)

            def negative_max(m):
                dve.wait_ge(*emptied(("mx", m, TB - 1, PAIRS - 1)))
                if m >= 1:
                    dve.wait_ge(*full(("shT", m - 1)))
                flat = nm[:, :, :, :].rearrange("p t a b -> p t (a b)")
                step(v.tensor_copy(shp[:, :, 0, :].bitcast(F32R), flat))
                v.tensor_tensor(shp[:, :, 1, :].bitcast(F32R), flat, shp[:, :, 0, :], ALU.subtract).then_inc(shp_ready, 1)

            def shift_rows(m):
                dve.wait_ge(*full(("shT", m)))
                if m >= 1:
                    dve.wait_ge(shift_in, 64 * m)
                v.tensor_copy(shs, bank(("shT", m))[0:4 * PAIRS, 0:L]).then_inc(ring_dve, 1)

            def split_heads(key):
                dve.wait_ge(*emptied(key))
                v.tensor_tensor(at_lo[:, :, :], at[:, :, :], at_hi[:, :, :], ALU.subtract)\
                 .then_inc(at_ready, 1)

            for step_ in ORDER:
                name, b = step_[0], step_[1] if len(step_) > 1 else None
                i_ = step_[2] if len(step_) > 2 else None
                tiles = [TB * b + i for i in range(TB)] if b is not None else []
                if name == "ada":
                    dve.wait_ge(silu_exp, 1)
                    step(v.tensor_scalar(silu[:, 1, :], silu[:, 0, :], 1.0, None, ALU.add))
                    step(v.reciprocal(silu[:, 0, :], silu[:, 1, :]))
                    v.tensor_tensor(silu[:, 2, :], silu[:, 0, :], col[:, 0:FC * B], ALU.mult).then_inc(silu_ready, 1)
                    dve.wait_ge(silu_ready, 1)
                    v.tensor_copy(srep, silu[:, 2, :].unsqueeze(2).to_broadcast([P, FC * B, P]))\
                     .then_inc(srep_ready, 1)
                    dve.wait_ge(s_row, 16)
                    v.tensor_scalar(sm[:, :], row[:, R_SML:R_SML + H0], LOG100, None, ALU.min).then_inc(sml_min, 1)
                    adaptive(("ada",), (0, 4), False)
                if name == "split_weights0":
                    for n, (hi, lo, src) in enumerate(((wqkv_hi, wqkv_lo, stage_b[:, 0:FC * 3 * C]),
                                                       (wp_hi, wp_lo, stage_b[:, FC * 3 * C:FC * 4 * C]))):
                        dve.wait_ge(w_hi, n + 1)
                        v.tensor_tensor(lo[:, :, :], src.rearrange("p (f n) -> p f n", f=FC), hi[:, :, :], ALU.subtract)\
                         .then_inc(w_lo_d, 1)
                if name == "ada_rest":
                    for s in range(2):
                        pair = kstk[:, s, :, :].rearrange("p (a c) n -> p a c n", c=2)
                        v.memset(pair[0:SLOT, :, 1, :].bitcast(F32), 0.0)
                        ins = v.memset(pair[SLOT:P, :, 0, :].bitcast(F32), 0.0)
                    ins.then_inc(kzero_ready, 1)
                    dve.wait_ge(s_bias, 16)
                    step(v.tensor_scalar(bias_sb[:, :, :], bias_sb[:, :, :], -3.0e38, None, ALU.max))
                    v.tensor_scalar(o_raw[:, 0, :], bias_sb[:, :, :].rearrange("p t n -> p (t n)"), 0.0, None,
                                    ALU.not_equal, ALU.add, accum_out=cnt[:, :]).then_inc(flag_ready, 1)
                    adaptive(("ada2",), (2, 6), True)
                    dve.wait_ge(*full(("flag",)))
                    v.tensor_copy(flag[:, :], bank(("flag",))[0:1, 0:1]).then_inc(ring_dve, 1)
                    for i in range(B):
                        dve.wait_ge(*full(("gam", i)))
                        v.tensor_tensor(gam[:, i, :], bank(("gam", i)), row[:, R_GAM:R_GAM + 2 * C], ALU.add)\
                         .then_inc(ring_dve, 1)
                if name == "stats0":
                    dve.wait_ge(s_x[b], 16)
                    statistics(0, b, xs)
                if name in ("norm0", "norm1", "norm2"):
                    normalise(int(name[-1]), b, x2 if name == "norm1" else xs)
                if name in ("split0", "split1", "split2"):
                    split_norm(int(name[-1]), b)
                if name == "qkv0":
                    for t in tiles:
                        dve.wait_ge(*full(("qk", t)))
                        if t >= TB:
                            dve.wait_ge(qn_ready, t - TB + 1)
                        v.tensor_tensor(qk[:, t % TB, :], bank(("qk", t)), row[:, R_QK:R_QK + 2 * C], ALU.add)\
                         .then_inc(ring_dve, 1)
                    dve.wait_ge(*full(("v", b)))
                    if b >= 3:
                        dve.wait_ge(pv_full, 4 * (b - 2))
                    if b == 0:
                        dve.wait_ge(const_ready, 3)
                    for i in range(TB):
                        ins = v.tensor_tensor(vs[:, b % 3, i, :, 0:D0],
                                              bank(("v", b))[:, i * C:(i + 1) * C].rearrange("p (a d) -> p a d", d=D0),
                                              row[:, R_V:R_V + C].rearrange("p (a d) -> p a d", d=D0), ALU.add)
                    ins.then_inc(ring_dve, 1)
                if name == "root0":
                    if b >= 1:
                        dve.wait_ge(rn_ready, b)
                    for t in tiles:
                        dve.wait_ge(sq_ready, t + 1)
                        step(v.tensor_reduce(ss[:, t % TB, :], qn[:, t % TB, :].rearrange("p (h d) -> p h d", d=D0),
                                             AX.X, ALU.add))
                    if b >= 1:
                        dve.wait_ge(qn_ready, TB * b)
                    seed(b, 2 * H0, v.tensor_scalar(ss[:, :, :], ss[:, :, :], 1e-24, None, ALU.max), seed_ready)
                if name == "unit0":
                    dve.wait_ge(rn_ready, b + 1)
                    for t in tiles:
                        v.tensor_tensor(qn[:, t % TB, :].rearrange("p (h d) -> p h d", d=D0),
                                        qk[:, t % TB, :].rearrange("p (h d) -> p h d", d=D0),
                                        rn[:, t % TB, :].unsqueeze(2).to_broadcast([P, 2 * H0, D0]), ALU.mult)\
                         .then_inc(qn_ready, 1)
                if name == "lo0":
                    for t in tiles:
                        dve.wait_ge(stk_hi_first, t + 1)
                        sr = stack[:, t % TB]
                        s = sr.bitcast(F32)
                        q = qn[:, t % TB, :].rearrange("p (h d) -> p h d", d=D0)
                        v.tensor_tensor(sr[:, 0:H0, 32:48], q[:, 0:H0], s[:, 0:H0, 0:16], ALU.subtract)
                        v.tensor_tensor(sr[:, H0:2 * H0, 16:32], q[:, H0:2 * H0], s[:, H0:2 * H0, 0:16], ALU.subtract)\
                         .then_inc(stk_lo, 1)
                if name == "max0":
                    for q in (2 * i_, 2 * i_ + 1):
                        row_max(b, q // PAIRS, q % PAIRS)
                if name == "neg0":
                    negative_max(b)
                if name == "shift0":
                    shift_rows(b)
                if name == "out0":
                    token_major_output(b, i_)
                if name == "heads0_lo":
                    split_heads(("aT", b))
                if name == "proj0":
                    dve.wait_ge(*full(("pj", b)))
                    gam1 = gam[:, b, 0:C].unsqueeze(1).to_broadcast([P, TB, C])
                    batch = slice(TB * b, TB * b + TB)
                    v.tensor_tensor(x2[:, batch, :], bank(("pj", b)).rearrange("p (t n) -> p t n", t=TB), gam1, ALU.mult)\
                     .then_inc(ring_dve, 1)
                    dve.wait_ge(*emptied(("pj", b)))
                    dve.wait_ge(xb_ready, b + 1)
                    v.tensor_tensor(x2[:, batch, :], x2[:, batch, :], xs[:, batch, :], ALU.add).then_inc(x2_ready, 1)
                if name == "stats1":
                    dve.wait_ge(x2_ready, b + 1)
                    statistics(1, b, x2)
                if name == "poly":
                    n = (HC // 2) * b + i_
                    dve.wait_ge(sq_u, n + 1)
                    v.scalar_tensor_tensor(gelu_z[:, n % 4, :], gelu_z[:, n % 4, :], 1.0 / GELU_A,
                                           gelu_u[:, n % 4, :], ALU.add, ALU.mult).then_inc(z_ready, 1)
                if name == "gelu":
                    n = (HC // 2) * b + i_
                    dve.wait_ge(t_ready, n + 1)
                    v.scalar_tensor_tensor(gelu_u[:, n % 4, :], gelu_z[:, n % 4, :], 1.0, gelu_u[:, n % 4, :],
                                           ALU.add, ALU.mult).then_inc(h_ready, 1)
                    dve.wait_ge(h_ready, n + 1)
                    if b == 0:
                        dve.wait_ge(s_full, PAIRS * B)
                    if b == 1:
                        dve.wait_ge(*full(("kT", NT - 1, 1)))
                    if b >= 2:
                        dve.wait_ge(*full(("f2", b - 2)))
                    v.tensor_copy(h_hi[b % 2][:, 2 * i_:2 * i_ + 2, :],
                                  gelu_u[:, n % 4, :].rearrange("p (a n) -> p a n", a=2)).then_inc(h_hi_ready, 1)
                if name == "fc2":
                    dve.wait_ge(*full(("f2", b)))
                    dve.wait_ge(x2b_ready, b + 1)
                    batch = slice(TB * b, TB * b + TB)
                    gam2 = gam[:, b, C:2 * C].unsqueeze(1).to_broadcast([P, TB, C])
                    v.scalar_tensor_tensor(x2[:, batch, :], bank(("f2", b)).rearrange("p (t n) -> p t n", t=TB), 0.5,
                                           gam2, ALU.mult, ALU.mult).then_inc(ring_dve, 1)
                    dve.wait_ge(*emptied(("f2", b)))
                    v.tensor_tensor(xs[:, batch, :], x2[:, batch, :], xs[:, batch, :], ALU.add).then_inc(x3_ready, 1)
                if name == "stats2":
                    dve.wait_ge(x3_ready, b + 1)
                    statistics(2, b, xs)
                if name == "root1":
                    if b >= 1:
                        dve.wait_ge(rn1_ready, b)
                    for t in tiles:
                        dve.wait_ge(sq1_ready, t + 1)
                        step(v.tensor_reduce(ss[:, t % TB, 0:2 * H1], qn[:, t % TB, :].rearrange("p (h d) -> p h d", d=D1),
                                             AX.X, ALU.add))
                    if b >= 1:
                        dve.wait_ge(rope_done, TB * b)
                    seed(b, 2 * H1, v.tensor_scalar(ss[:, :, 0:2 * H1], ss[:, :, 0:2 * H1], 1e-6, None, ALU.add),
                         seed1_ready)
                if name == "rope":
                    for t in tiles:
                        x_ = qk[:, t % TB, :].rearrange("p (g d) -> p g d", d=D1 // 2)
                        bb = rope_b[:, t % 2, :].rearrange("p (g d) -> p g d", d=D1 // 2)
                        if t == 0:
                            dve.wait_ge(s_rope, 16)
                            dve.wait_ge(w_lo_p, 3)
                            dve.wait_ge(w_hi, 5)
                        dve.wait_ge(*emptied(("qk1", t)))
                        step(v.tensor_tensor(bb, x_, rope_sb[:, t % TB, 1:2, :].to_broadcast([P, 4 * H1, D1 // 2]), ALU.mult))
                        dve.wait_ge(cos_done, t + 1)
                        a4 = rope_a[:, t % 2, :].rearrange("p (h s d) -> p h s d", s=2, d=D1 // 2)
                        b4 = rope_b[:, t % 2, :].rearrange("p (h s d) -> p h s d", s=2, d=D1 // 2)
                        r4 = qn[:, t % TB, :].rearrange("p (h s d) -> p h s d", s=2, d=D1 // 2)
                        v.tensor_tensor(r4[:, :, 0, :], a4[:, :, 0, :], b4[:, :, 1, :], ALU.subtract)
                        step(v.tensor_tensor(r4[:, :, 1, :], a4[:, :, 1, :], b4[:, :, 0, :], ALU.add))
                        dve.wait_ge(rn1_ready, b + 1)
                        r = qn[:, t % TB, :].rearrange("p (h d) -> p h d", d=D1)
                        v.tensor_tensor(r, r, rn[:, t % TB, 0:2 * H1].unsqueeze(2).to_broadcast([P, 2 * H1, D1]), ALU.mult)\
                         .then_inc(rope_done, 1)
                if name == "lo1":
                    for t in tiles:
                        dve.wait_ge(stk1_hi_first, t + 1)
                        sr = stk1[:, t % TB]
                        s = sr.bitcast(F32)
                        r = qn[:, t % TB, :].rearrange("p (h d) -> p h d", d=D1)
                        v.tensor_tensor(sr[:, 0:H1, D1:2 * D1], r[:, 0:H1], s[:, 0:H1, 0:D1], ALU.subtract)
                        for i in range(2):
                            ins = v.tensor_tensor(sr[:, 2 * H1:3 * H1, i * D1:(i + 1) * D1], r[:, H1:2 * H1],
                                                  s[:, H1:2 * H1, 0:D1], ALU.subtract)
                        ins.then_inc(stk1_lo, 1)
                if name == "max1":
                    for hp in range(2):
                        key = ("mx1", b, i_, hp)
                        dve.wait_ge(*full(key))
                        v.tensor_reduce(nm1[:, i_, 2 * hp:2 * hp + 2], bank(key).rearrange("p (h n) -> p h n", h=2),
                                        AX.X, ALU.max, negate=True).then_inc(ring_dve, 1)
                if name == "neg1":
                    dve.wait_ge(*emptied(("mx1", b, TB - 1, 1)))
                    if b >= 1:
                        dve.wait_ge(*full(("shT1", b - 1)))
                    step(v.tensor_copy(sh1[:, :, 0:H1].bitcast(F32R), nm1[:, :, :]))
                    v.tensor_tensor(sh1[:, :, H1:2 * H1].bitcast(F32R), nm1[:, :, :], sh1[:, :, 0:H1], ALU.subtract)\
                     .then_inc(sh1_ready, 1)
                if name == "shift1":
                    dve.wait_ge(*full(("shT1", b)))
                    if b == 0:
                        dve.wait_ge(const_ready, 4)
                    else:
                        dve.wait_ge(s_full, PAIRS * B + 2 * b)
                    v.tensor_copy(shs1[0:2 * H1, :], bank(("shT1", b))[0:2 * H1, 0:L]).then_inc(ring_dve, 1)
                if name == "out1":
                    key = ("sT1", b)
                    dve.wait_ge(*full(key))
                    dve.wait_ge(*emptied(("oT", B - 1, 1) if b == 0 else ("oT1", b - 1)))
                    rs = bank(key)[:, 0:TB * P].rearrange("p (t h s) -> p t h s", t=TB, h=H1)
                    v.reciprocal(rv[:, 0:TB, :], rs[:, :, :, 0]).then_inc(ring_dve, 1)
                    dve.wait_ge(*emptied(key))
                    key = ("oT1", b)
                    dve.wait_ge(*full(key))
                    dve.wait_ge(*full(("aT", B - 1) if b == 0 else ("aT1", b - 1)))
                    src = bank(key).rearrange("p (h q i d) -> p h q i d", h=2, q=TB, i=2)
                    ot = o_tok[:, :, :].rearrange("p t (h d) -> p t h d", d=D1)
                    for hp in range(2):
                        ins = v.tensor_tensor(ot[:, :, 2 * hp:2 * hp + 2, :], src[:, hp],
                                              rv[:, 0:TB, 2 * hp:2 * hp + 2].unsqueeze(3).to_broadcast([P, TB, 2, D1]),
                                              ALU.mult)
                    ins.then_inc(ring_dve, 1)
                if name == "heads1_lo":
                    split_heads(("aT1", b))
                if name == "proj1":
                    dve.wait_ge(*full(("po", b)))
                    batch = slice(TB * b, TB * b + TB)
                    v.tensor_tensor(x2[:, batch, :], bank(("po", b)).rearrange("p (t n) -> p t n", t=TB), xs[:, batch, :],
                                    ALU.add).then_inc(ring_dve, 1)


_INS = ["x", "wqkv", "wproj", "wada", "wfc1", "wfc2", "wnorm", "wqkv1", "wout1", "cols", "rows", "rope", "bias", "mask"]


def kernel(x, cond_2048, pos_BxS, mask_1x1xSxS_ff0, mask_Bx1xSxS_bf1, L0_cond_Wqkv, L0_cond_q_bias, L0_cond_v_bias,
           L0_cond_scale_mul_log, L0_cond_Wproj, L0_cond_bproj, L0_cond_Wada, L0_cond_bada, L0_cond_Wfc1, L0_cond_bfc1,
           L0_cond_Wfc2, L0_cond_bfc2, L1_cond_norm_w, L1_cond_qkv_w, L1_cond_scale, L1_cond_out_w):
    import concourse.bacc as _bacc
    from concourse.bass_utils import run_bass_kernel_spmd as _run

    def arr(a):
        return np.asarray(a)

    def columns(a, n):
        return arr(a).reshape(n, P).T

    cond = arr(cond_2048)
    cols = np.concatenate([cond.reshape(B, FC, P).transpose(2, 1, 0).reshape(P, FC * B),
                           columns(arr(L0_cond_bada)[2 * C:], 8), columns(L0_cond_bfc1, HC)], axis=1)
    rows = np.concatenate([arr(L0_cond_q_bias), np.zeros(C, np.float32), arr(L0_cond_v_bias), arr(L0_cond_bproj),
                           arr(L0_cond_bfc2), arr(L0_cond_bada)[:2 * C], arr(L0_cond_scale_mul_log).reshape(-1),
                           arr(L1_cond_scale)])[None, :]
    half = D1 // 2
    inv_freq = (np.float32(1.0) / np.float32(10000.0) ** (np.arange(half, dtype=np.float32) / np.float32(half)))
    theta = np.arange(L, dtype=np.float32)[:, None] * inv_freq.astype(np.float32)[None, :]
    rope = np.stack([np.cos(theta), np.sin(theta)], axis=1).astype(np.float32)
    given = {
        "x": arr(x).reshape(B * L, C), "wqkv": arr(L0_cond_Wqkv).T, "wproj": arr(L0_cond_Wproj).T,
        "wada": arr(L0_cond_Wada).T, "wfc1": arr(L0_cond_Wfc1).T, "wfc2": arr(L0_cond_Wfc2).T,
        "wnorm": arr(L1_cond_norm_w).T, "wqkv1": arr(L1_cond_qkv_w).T, "wout1": arr(L1_cond_out_w).T,
        "cols": cols, "rows": rows, "rope": rope, "bias": arr(mask_1x1xSxS_ff0).reshape(L, L),
        "mask": arr(mask_Bx1xSxS_bf1).reshape(B, L, L).view(np.uint8),
    }
    nc = _bacc.Bacc("TRN2", target_bir_lowering=False, num_devices=1)
    arrays, args = {}, []
    for name in _INS:
        a = np.ascontiguousarray(given[name])
        arrays[f"in_{name}"] = a
        args.append(nc.dram_tensor(f"in_{name}", a.shape, mybir.dt.from_np(a.dtype), kind="ExternalInput").ap())
    out = nc.dram_tensor("out_0", (B * L, C), F32, kind="ExternalOutput").ap()
    build(nc, *args, out)
    r = _run(nc, [arrays], core_ids=[0])
    return r.results[0]["out_0"].reshape(B, L, C)
```

```python
from contextlib import ExitStack

import numpy as np

import concourse.bass as bass
from concourse import mybir

F32 = mybir.dt.float32
F32R = mybir.dt.float32r
BF16 = mybir.dt.bfloat16
I32 = mybir.dt.int32
ALU = mybir.AluOpType
ACT = mybir.ActivationFunctionType
AX = mybir.AxisListType

P = 128
B, L, C = 4, 256, 256
NT = B * L // P
TB = L // P
FC = C // P
H0, D0 = 16, C // 16
PAIRS = H0 // 2
SLOT = 64
H1, D1 = 4, C // 4
HID = 4 * C
HC = HID // P
LN_EPS = 1e-6
LOG100 = float(np.log(np.float32(100.0)))
GELU_C = float(np.sqrt(2.0 / np.pi))
GELU_A = 0.044715
NEG = -1e30
RING = 3

R_QK, R_V, R_PF, R_GAM, R_SML, R_SC = 0, 512, 768, 1280, 1792, 1808
R_END = 1812



ORDER = [(name, *map(int, filter(None, rest.split(".")))) for name, _, rest in (word.partition(":") for word in """
zeros:0 silu split_wqkv0 head_scales stats0:0 ada zeros:1 normed0:0 norm0:0 stats0:1 split0:0 const_stack
norm0:1 bias_count qk0:0.0 const_v square0:0.0 stats0:2 qk0:0.1 norm0:2 square0:0.1 root0:0 normed0:1 sums0:0
gamma_rows flag ada_rest normed0:2 split0:1 const_sel v0:0 unit0:0.0 hi0:0.0 unit0:0.1 hi0:0.1 lo0:0.0 qk0:1.0
qk0:1.1 square0:1.0 square0:1.1 turnk0:0.0 lo0:0.1 stats0:3 turnq0:0.0 turnk0:0.1 root0:1 turnq0:0.1 gamma:0
split0:2 square0:2.0 sums0:1 gamma:1 square0:2.1 norm0:3 root0:2 max0:0.0 max0:0.1 max0:0.2 max0:0.3 mask
unit0:1.0 xbias0:0 unit0:1.1 hi0:1.0 max0:0.4 lo0:1.0 hi0:1.1 qk0:2.0 max0:0.5 max0:0.6 split_wproj qk0:2.1
turnq0:1.0 lo0:1.1 max0:0.7 normed0:3 turnk0:1.0 neg0:0 sums0:2 v0:1 turnq0:1.1 shift0:0 split0:3 turnk0:1.1
v0:2 gamma:2 max0:1.0 score0:0.0 score0:0.1 unit0:2.0 max0:1.1 square0:3.0 score0:0.2 max0:1.2 max0:1.3
unit0:2.1 hi0:2.0 score0:0.3 square0:3.1 max0:1.4 value0:0.0 score0:0.4 max0:1.5 score0:0.5 max0:1.6 take0:0.0
value0:0.1 max0:1.7 neg0:1 score0:0.6 lo0:2.0 qk0:3.0 hi0:2.1 score0:0.7 lo0:2.1 shift0:1 qk0:3.1 turnk0:2.0
sums0:3 value0:0.2 turnk0:2.1 root0:3 out0:0.0 score0:1.0 take0:0.1 xbias1:0 value0:0.3 turnq0:2.0 score0:1.1
v0:3 turnq0:2.1 score0:1.2 unit0:3.0 hi0:3.0 unit0:3.1 out0:0.1 gamma:3 score0:1.3 max0:2.0 lo0:3.0 hi0:3.1
value0:1.0 max0:2.1 score0:1.4 max0:2.2 value0:1.1 heads0:0 take0:1.0 max0:2.3 score0:1.5 max0:2.4 score0:1.6
max0:2.5 score0:1.7 max0:2.6 value0:1.2 max0:2.7 neg0:2 turnq0:3.0 lo0:3.1 heads0_lo:0 turnk0:3.0 shift0:2
proj0:0 turnq0:3.1 turnk0:3.1 out0:1.0 score0:2.0 value0:1.3 xbias0:1 stats1:0 score0:2.1 take0:1.1 max0:3.0
score0:2.2 max0:3.1 norm1:0 score0:2.3 value0:2.0 max0:3.2 score0:2.4 max0:3.3 score0:2.5 max0:3.4 take0:2.0
out0:1.1 max0:3.5 value0:2.1 max0:3.6 score0:2.6 score0:2.7 max0:3.7 value0:2.2 neg0:3 heads0:1 shift0:3
split_w1 normed1:0 heads0_lo:1 value0:2.3 out0:2.0 take0:2.1 proj0:1 score0:3.0 out0:2.1 score0:3.1 score0:3.2
heads0:2 stats1:1 split1:0 norm1:1 score0:3.3 xbias1:1 heads0_lo:2 value0:3.0 score0:3.4 xbias0:2 score0:3.5
take0:3.0 value0:3.1 normed1:1 score0:3.6 xbias1:2 score0:3.7 proj0:2 stats1:2 value0:3.2 split_w2 split_wqkv1
take0:3.1 hlo:0.0 split1:1 out0:3.0 value0:3.3 fc1:0.0 hlo:0.1 fc1:0.1 poly:0.0 hlo:0.2 xbias0:3 tanh:0.0
out0:3.1 norm1:2 fc1:0.2 fc1:0.3 gelu:0.0 tanh:0.1 heads0:3 poly:0.1 hlo:0.3 tanh:0.2 normed1:2 fc1:1.0
poly:0.2 hlo:1.0 tanh:0.3 poly:0.3 gelu:0.1 fc1:1.1 heads0_lo:3 gelu:0.2 split1:2 poly:1.0 fc1:1.2 gelu:0.3
poly:1.1 split_wout1 proj0:3 tanh:1.0 poly:1.2 gelu:1.0 stats1:3 hlo:1.1 tanh:1.1 fc1:1.3 gelu:1.1 tanh:1.2
fc1:2.0 poly:1.3 hlo:1.2 gelu:1.2 tanh:1.3 gelu:1.3 fc2:0 hlo:1.3 fc1:2.1 norm1:3 poly:2.0 fc1:2.2 poly:2.1
stats2:0 tanh:2.0 hlo:2.0 fc1:2.3 gelu:2.0 hlo:2.1 tanh:2.1 xbias1:3 poly:2.2 poly:2.3 norm2:0 split1:3
gelu:2.1 split2:0 normed1:3 tanh:2.2 fc2:1 normed2:0 hlo:2.2 gelu:2.2 square1:0.0 stats2:1 cos:0.0 poly:3.0
gelu:2.3 poly:3.1 gelu:3.0 tanh:2.3 fc1:3.0 qk1:0.0 fc1:3.1 v1:0 hlo:2.3 square1:0.1 gelu:3.1 hlo:3.0 norm2:1
tanh:3.0 hlo:3.1 tanh:3.1 root1:0 poly:3.2 hlo:3.2 rsums1:0 qk1:0.1 fc1:3.2 gelu:3.2 hlo:3.3 fc1:3.3 tanh:3.2
normed2:1 poly:3.3 cos:0.1 split2:1 gelu:3.3 rope:0.0 tanh:3.3 cos:1.0 fc2:2 stats2:2 qk1:1.0 rope:0.1 norm2:2
hi1:0.0 fc2:3 lo1:0.0 v1:1 stats2:3 lo1:0.1 norm2:3 square1:1.0 normed2:2 hi1:0.1 square1:1.1 qk1:1.1 root1:1
turn1:0.0 split2:2 rsums1:1 turn1:0.1 max1:0.0 max1:0.1 cos:1.1 neg1:0 hi1:1.0 rope:1.0 qk1:2.0 shift1:0
rope:1.1 hi1:1.1 qk1:2.1 cos:2.0 square1:2.0 score1:0.0 v1:2 normed2:3 lo1:1.0 square1:2.1 score1:0.1 turn1:1.0
lo1:1.1 rsums1:2 cos:2.1 sum1:0 split2:3 turn1:1.1 qk1:3.0 rope:2.0 hi1:2.0 hi1:2.1 rope:2.1 lo1:2.0 value1:0
max1:1.0 root1:2 qk1:3.1 lo1:2.1 rsums1:3 turn1:2.0 square1:3.0 turn1:2.1 max1:1.1 square1:3.1 neg1:1 v1:3
cos:3.0 max1:2.0 shift1:1 max1:2.1 rope:3.0 hi1:3.0 cos:3.1 neg1:2 score1:1.0 out1:0 score1:1.1 lo1:3.0
shift1:2 heads1:0 hi1:3.1 score1:2.0 rope:3.1 heads1_lo:0 sum1:1 lo1:3.1 turn1:3.0 root1:3 value1:1 turn1:3.1
score1:2.1 max1:3.0 max1:3.1 neg1:3 sum1:2 out1:1 shift1:3 proj1:0 score1:3.0 heads1_lo:1 value1:2 heads1:1
score1:3.1 out1:2 heads1_lo:2 proj1:1 sum1:3 heads1:2 value1:3 out1:3 proj1:2 heads1_lo:3 heads1:3 proj1:3
""".split())]
FIRST_SCORE = min(i for i, step in enumerate(ORDER) if step[0] == "max0")
AFTER_SCORES = max(i for i, step in enumerate(ORDER) if step[0] == "score0") + 1


def units_of(step):
    name, b = step[0], step[1] if len(step) > 1 else None
    i = step[2] if len(step) > 2 else None
    tiles = [TB * b + t for t in range(TB)] if b is not None else []
    if name == "ada":
        return [(("ada",), "dve")]
    if name == "ada_rest":
        return [(("ada2",), "dve")]
    if name == "flag":
        return [(("flag",), "dve")]
    if name == "gamma_rows":
        return [(("gam_rows",), "dve")]
    if name == "gamma":
        return [(("gam", b), "act")]
    if name in ("normed0", "normed1", "normed2"):
        return [(("xT", int(name[-1]), b), "act")]
    if name == "qk0":
        return [(("qk", tiles[i]), "dve")]
    if name == "v0":
        return [(("v", b), "dve")]
    if name in ("turnq0", "turnk0"):
        return [((name[4] + "T", tiles[i], u), "act") for u in range(2)]
    if name == "max0":
        return [(("mx", b, q // PAIRS, q % PAIRS), "dve") for q in (2 * i, 2 * i + 1)]
    if name == "shift0":
        return [(("shT", b), "dve")]
    if name == "out0":
        return [(("oT", b, i), "dve")]
    if name == "heads0":
        return [(("aT", b), "act")]
    if name == "proj0":
        return [(("pj", b), "dve")]
    if name == "fc1":
        return [(("f1", b, i), "act")]
    if name == "fc2":
        return [(("f2", b), "dve")]
    if name == "qk1":
        return [(("qk1", tiles[i]), "act")]
    if name == "v1":
        return [(("v1", b), "act")]
    if name == "turn1":
        return [((w, tiles[i]), "act") for w in ("q1T", "k1T0", "k1T1")]
    if name == "max1":
        return [(("mx1", b, i, hp), "dve") for hp in range(2)]
    if name == "shift1":
        return [(("shT1", b), "dve")]
    if name == "out1":
        return [(("sT1", b), "dve"), (("oT1", b), "dve")]
    if name == "heads1":
        return [(("aT1", b), "act")]
    if name == "proj1":
        return [(("po", b), "dve")]
    return []


class Ring:

    def __init__(self, order):
        self.number, self.emptied = {}, {}
        counts = {"dve": 0, "act": 0}
        for step in order:
            for key, engine in units_of(step):
                assert key not in self.number, key
                self.number[key] = len(self.number)
                counts[engine] += 1
                self.emptied[key] = (engine, counts[engine])
        self.keys = list(self.number)


def positions(order, kinds):
    out = {}
    for step in order:
        if step[0] in kinds:
            out[(kinds.index(step[0]), step[1])] = len(out)
    return out


def build(nc, x, wqkv, wproj, wada, wfc1, wfc2, wnorm, wqkv1, wout1, cols, rows, rope, bias, mask, out):
    ring_plan = Ring(ORDER)
    stat_no = positions(ORDER, ["stats0", "stats1", "stats2"])
    norm_keys = [key[1:] for key in ring_plan.keys if key[0] == "xT"]
    norm_no = {key: n for n, key in enumerate(norm_keys)}

    with ExitStack() as ctx:
        def sb(name, shape, dt=F32):
            return ctx.enter_context(nc.sbuf_tensor(name, shape, dt))

        def sem(name):
            return ctx.enter_context(nc.semaphore(name))

        xs = sb("xs", [P, NT, C])
        x2 = sb("x2", [P, NT, C])
        wqkv_hi, wqkv_lo = (sb(n, [P, FC, 3 * C], F32R) for n in ("wqkv_hi", "wqkv_lo"))
        wp_hi, wp_lo = (sb(n, [P, FC, C], F32R) for n in ("wp_hi", "wp_lo"))
        wo_hi, wo_lo = (sb(n, [P, FC, C], F32R) for n in ("wo_hi", "wo_lo"))
        stage_a = sb("stage_a", [P, FC * 6 * C])
        stage_b = sb("stage_b", [P, 2048])
        gam = sb("gam", [P, B, 2 * C])
        stack = sb("stack", [P, TB, 2 * H0, SLOT], F32R)
        qstk = sb("qstk", [P, 2, PAIRS, L], F32R)
        kstk = sb("kstk", [P, 2, H0, L], F32R)
        vs = sb("vs", [P, 3, TB, H0, 32])
        ps = sb("ps", [P, 4, 2, TB, L])
        xh = sb("xh", [P, TB, C])
        xmt = sb("xmt", [P, FC, L])
        xm_hi, xm_lo = (sb(n, [P, 2, FC, L], F32R) for n in ("xm_hi", "xm_lo"))
        qk = sb("qk", [P, TB, 2 * C])
        qn = sb("qn", [P, TB, 2 * C])
        o_raw = sb("o_raw", [P, 2, 2 * L])
        o_tok = sb("o_tok", [P, TB, C])
        at_hi, at_lo = (sb(n, [P, FC, L], F32R) for n in ("at_hi", "at_lo"))
        row = sb("row", [P, R_END])
        col = sb("col", [P, 24])
        rope_sb = sb("rope_sb", [P, TB, 2, D1 // 2])
        bias_sb = sb("bias_sb", [P, TB, L])
        mask_add = sb("mask_add", [P, B, TB, L], BF16)
        ident = sb("ident", [P, P])
        ident_b = sb("ident_b", [P, P], BF16)
        ones = sb("ones", [P, 32])
        sel = sb("sel", [P, H1, P], F32R)
        silu = sb("silu", [P, 3, FC * B])
        silu2 = sb("silu2", [P, FC, 2 * B])
        mod = sb("mod", [P, 10, B])
        sm = sb("sm", [P, H0])
        sqs = sb("sqs", [P, 2 * H1])
        half_neg = sb("half_neg", [P, TB])
        half_pos = sb("half_pos", [P, H1])
        bnst = sb("bnst", [P, 3, B, TB, 6])
        mv = sb("mv", [P, 3, B, TB, 2])
        ve = sb("ve", [P, 3, B, TB])
        rstd = sb("rstd", [P, 3, B, TB])
        zero_col = sb("zero_col", [P, 1])
        ss = sb("ss", [P, TB, 2 * H0])
        rn = sb("rn", [P, TB, 2 * H0])
        nt = sb("nt", [P, TB, 2 * H0])
        nm = sb("nm", [P, TB, 2, PAIRS])
        shp = sb("shp", [P, TB, 2, 2, PAIRS])
        sh1 = sb("sh1", [P, TB, 2 * H1])
        shs1 = sb("shs1", [P, L], F32R)
        rv = sb("rv", [P, 4, 4])
        nm1 = sb("nm1", [P, TB, H1])
        cnt = sb("cnt", [P, 1])
        flag = sb("flag", [1, 1], I32)

        term = stage_a[:, 2048:2048 + C]
        at = stage_a[:, 2304:2304 + FC * L].rearrange("p (f n) -> p f n", f=FC)
        shs = stage_a[0:4 * PAIRS, 2816:2816 + L]
        wnorm_sb = gam[:, 0, :].rearrange("p (f n) -> p f n", f=FC)
        mask_u8 = o_tok[:, :, :].rearrange("p t n -> p (t n)").bitcast(mybir.dt.uint8)\
            .rearrange("p (b t k) -> p b t k", b=B, t=TB)
        sel_f = o_raw[:, 1, :].rearrange("p (h n) -> p h n", h=H1)
        gam_rows = o_raw[0:2 * B, 0, :]
        wada_sb = stage_a[:, :].rearrange("p (f n) -> p f n", f=FC)
        rope_a = stage_a[:, 0:1024].rearrange("p (t n) -> p t n", t=2)
        rope_b = stage_a[:, 1024:2048].rearrange("p (t n) -> p t n", t=2)
        stack_flat = stack[:, :, :, :].rearrange("p t h s -> p t (h s)")
        h_hi = (qstk[:, 0], stack_flat[:, 0].rearrange("p (c n) -> p c n", c=HC))
        h_lo = (qstk[:, 1], stack_flat[:, 1].rearrange("p (c n) -> p c n", c=HC))
        w1_hi = kstk[:, 0, 0:8, :].rearrange("p a b -> p (a b)").rearrange("p (f n) -> p f n", f=FC)
        w1_lo = kstk[:, 0, 8:16, :].rearrange("p a b -> p (a b)").rearrange("p (f n) -> p f n", f=FC)
        w2_hi = kstk[:, 1, 0:8, :]
        w2_lo = kstk[:, 1, 8:16, :]
        gelu_u = ps[:, 0:2].rearrange("p c a b n -> p (c a b n)").rearrange("p (s n) -> p s n", s=4)
        gelu_z = ps[:, 2:4].rearrange("p c a b n -> p (c a b n)").rearrange("p (s n) -> p s n", s=4)
        k1 = kstk[:, 0, :, :].rearrange("p (s w h) n -> p s w h n", s=2, w=2)
        q1 = kstk[:, 1, 0:8, :].rearrange("p (s h) n -> p s h n", s=2)
        stk1 = stack_flat[:, :, 0:12 * P]\
            .rearrange("p t (g n) -> p t g n", g=12)
        v1 = vs[:, :, :, :, :].rearrange("p s t h d -> p s t (h d)")[:, :, :, 0:C]

        psx = ctx.enter_context(nc.psum_tensor("psx", [P, 2, 2, TB, L], F32))
        ring = ctx.enter_context(nc.psum_tensor("ring", [P, RING, 512], F32))
        pv = ctx.enter_context(nc.psum_tensor("pv", [P, 512], F32))

        s_col, s_row, s_bias, s_mask, s_rope, s_norm, s_wada, s_wada2, s_wq, s_wp, s_w1, s_w2, s_wq1, s_wo = (
            sem(f"in_{n}") for n in ("col", "row", "bias", "mask", "rope", "norm", "wada", "wada_rest", "wq", "wp",
                                     "w1", "w2", "wq1", "wo"))
        s_x = [sem(f"in_x{b}") for b in range(B)]
        mask_ready = sem("mask_ready")
        kzero_ready = sem("k_stack_zeros_ready")
        const_ready = sem("const_ready")
        ring_full = sem("ring_full")
        ring_dve, ring_act = sem("ring_emptied_by_vector"), sem("ring_emptied_by_scalar")
        silu_exp, silu_ready, silu2_ready = sem("silu_exp"), sem("silu_ready"), sem("silu_twice_ready")
        rows_hi, rows_ready = sem("gamma_rows_added"), sem("gamma_rows_ready")
        sml_min = sem("scale_mul_log_clamped")
        mod_ready = sem("mod_ready")
        scales_ready = sem("scales_ready")
        flag_ready = sem("flag_ready")
        w_hi, w_lo_d, w_lo_p = sem("weights_hi"), sem("weights_lo_vector"), sem("weights_lo_pool")
        xb_ready = sem("x_bias_ready")
        x2_ready, x2b_ready, x3_ready = sem("x2_ready"), sem("x2_bias_ready"), sem("x3_ready")
        stats_ready, rstd_ready = sem("stats_ready"), sem("rstd_ready")
        xh_ready, xmt_ready, xm_ready = sem("xh_ready"), sem("xmt_ready"), sem("xm_ready")
        sq_ready, seed_ready, rn_ready = sem("sq_ready"), sem("seed_ready"), sem("rn_ready")
        qn_ready, stk_hi, stk_lo = sem("qn_ready"), sem("stack_hi"), sem("stack_lo")
        stk_hi_first, stk1_hi_first = sem("stack_hi_first"), sem("stack1_hi_first")
        nm_ready, shp_ready, shift_in = sem("negmax_ready"), sem("shift_ready"), sem("shift_in")
        s_full, exp_done = sem("scores_full"), sem("exp_done")
        pv_full, pv_taken = sem("pv_full"), sem("pv_taken")
        at_ready = sem("heads_ready")
        sq1_ready, seed1_ready, rn1_ready = sem("sq1_ready"), sem("seed1_ready"), sem("rn1_ready")
        cos_done, rope_done = sem("cos_done"), sem("rope_done")
        stk1_hi, stk1_lo = sem("stack1_hi"), sem("stack1_lo")
        sh1_ready = sem("shift1_ready")
        sq_u, z_ready, t_ready, h_ready, h_hi_ready, h_lo_ready = (
            sem(n) for n in ("gelu_square", "gelu_poly", "gelu_tanh", "gelu_out", "h_hi_ready",
                             "h_lo_ready"))
        s_out = sem("out_stored")
        dve_step, pool_step = sem("vector_step"), sem("pool_step")
        block = ctx.enter_context(nc.Block())

        def full(key):
            return ring_full, ring_plan.number[key] + 1

        def emptied(key):
            engine, value = ring_plan.emptied[key]
            return (ring_dve if engine == "dve" else ring_act), value

        def bank(key):
            return ring[:, ring_plan.number[key] % RING, :]

        def previous_in_bank(key):
            n = ring_plan.number[key] - RING
            return ring_plan.keys[n] if n >= 0 else None

        def stepper(eng, s):
            count = [0]

            def step(ins):
                count[0] += 1
                ins.then_inc(s, 1)
                eng.wait_ge(s, count[0])
            return step

        def last_matmul_of_norm(kind, b):
            return [("v", b), ("f1", b, HC // 2 - 1), ("v1", b)][kind]


        @block.sync
        def _(sp):
            x_v = x.rearrange("(t p) c -> p t c", p=P)

            def load_x(b):
                sp.dma_start(xs[:, TB * b:TB * b + TB, :], x_v[:, TB * b:TB * b + TB, :])\
                  .then_inc(s_x[b], 16)

            sp.dma_start(col[:, :], cols).then_inc(s_col, 16)
            load_x(0)
            wada_v = wada.rearrange("(f p) n -> p f n", p=P)

            def load_wada(a, b_, arrived):
                sp.dma_start(wada_sb[:, :, a:b_], wada_v[:, :, a:b_]).then_inc(arrived, 16)

            load_wada(2 * C, 3 * C, s_wada)
            load_wada(4 * C, 5 * C, s_wada)
            sp.dma_start(stage_b[:, 0:FC * 3 * C].rearrange("p (f n) -> p f n", f=FC),
                         wqkv.rearrange("(f p) n -> p f n", p=P)).then_inc(s_wq, 16)
            sp.dma_start(row[:, :], rows.to_broadcast([P, R_END])).then_inc(s_row, 16)
            load_wada(3 * C, 4 * C, s_wada2)
            load_wada(5 * C, 6 * C, s_wada2)
            load_wada(0, 2 * C, s_wada2)
            sp.dma_start(wnorm_sb, wnorm.rearrange("(f p) n -> p f n", p=P)).then_inc(s_norm, 16)
            load_x(1)
            sp.dma_start(stage_b[:, FC * 3 * C:FC * 4 * C].rearrange("p (f n) -> p f n", f=FC),
                         wproj.rearrange("(f p) n -> p f n", p=P)).then_inc(s_wp, 16)
            load_x(2)
            load_x(3)
            sp.dma_start(bias_sb[:, :, :], bias.rearrange("(t p) k -> p t k", p=P)).then_inc(s_bias, 16)
            sp.dma_start(rope_sb[:, :, :, :], rope.rearrange("(t p) s d -> p t s d", p=P)).then_inc(s_rope, 16)
            sp.dma_start(mask_u8, mask.rearrange("b (t p) k -> p b t k", p=P)).then_inc(s_mask, 16)
            def shift_rows(b):
                sp.wait_ge(*emptied(("shT", b)))
                for par in range(2):
                    sp.dma_start(qstk[SLOT * par + 48:SLOT * par + 50, b % 2, :, :].bitcast(F32),
                                 shs[2 * PAIRS * par:2 * PAIRS * (par + 1), :]).then_inc(shift_in, 16)

            shift_rows(0)
            sp.wait_ge(*full(("gam_rows",)))
            sp.wait_ge(*emptied(("ada2",)))
            sp.dma_start(stage_a[:, 0:FC * HID].rearrange("p (f n) -> p f n", f=FC),
                         wfc1.rearrange("(f p) n -> p f n", p=P)).then_inc(s_w1, 16)
            sp.wait_ge(w_hi, 2)
            sp.wait_ge(w_lo_d, 2)
            sp.dma_start(stage_b[:, :].rearrange("p (f n) -> p f n", f=HC),
                         wfc2.rearrange("(f p) n -> p f n", p=P)).then_inc(s_w2, 16)

            for b in range(1, B):
                shift_rows(b)
            sp.wait_ge(w_hi, 3)
            sp.wait_ge(w_lo_p, 1)
            sp.dma_start(stage_a[:, 0:FC * 3 * C].rearrange("p (f n) -> p f n", f=FC),
                         wqkv1.rearrange("(f p) n -> p f n", p=P)).then_inc(s_wq1, 16)
            sp.wait_ge(w_hi, 4)
            sp.wait_ge(w_lo_p, 2)
            sp.dma_start(stage_b[:, 0:FC * C].rearrange("p (f n) -> p f n", f=FC),
                         wout1.rearrange("(f p) n -> p f n", p=P)).then_inc(s_wo, 16)
            out_v = out.rearrange("(t p) c -> p t c", p=P)
            for b in range(B):
                sp.wait_ge(*emptied(("po", b)))
                sp.dma_start(out_v[:, TB * b:TB * b + TB, :], x2[:, TB * b:TB * b + TB, :]).then_inc(s_out, 16)
            sp.wait_ge(s_out, 16 * B)

        @block.gpsimd
        def _(pool):
            g = nc.gpsimd
            step = stepper(pool, pool_step)
            g.memset(half_neg[:, :], -0.5)
            g.memset(half_pos[:, :], 0.5)
            g.memset(zero_col[:, :], 0.0)
            step(g.memset(ident[:, :], 0.0))
            step(g.affine_select(out=ident[:, :], in_=ident[:, :], compare_op=ALU.not_equal, fill=1.0, base=0,
                                 pattern=[[-1, P]], channel_multiplier=1))
            g.tensor_copy(ident_b[:, :], ident[:, :])
            g.memset(ones[:, :], 1.0).then_inc(const_ready, 1)
            def rstd_of(kind, b):
                pool.wait_ge(stats_ready, stat_no[(kind, b)] + 1)
                g.tensor_tensor(rstd[:, kind, b, :], ve[:, kind, b, :], half_neg[:, 0:TB], ALU.pow)\
                 .then_inc(rstd_ready, 1)

            def inverse_root(seeded, b, n):
                pool.wait_ge(seeded, b + 1)
                y, x_, t = rn[:, :, 0:n], ss[:, :, 0:n], nt[:, :, 0:n]
                for _ in range(3):
                    step(g.tensor_tensor(t, x_, y, ALU.mult))
                    step(g.tensor_tensor(t, t, y, ALU.mult))
                    step(g.tensor_scalar(t, t, -0.5, 1.5, ALU.mult, ALU.add))
                    step(g.tensor_tensor(y, y, t, ALU.mult))

            for step_ in ORDER:
                name, b = step_[0], step_[1] if len(step_) > 1 else None
                i_ = step_[2] if len(step_) > 2 else None
                if name == "const_stack":
                    step(g.memset(stack[:, :, :, 48:64].bitcast(F32), 0.0))
                    g.memset(stack[:, :, H0:2 * H0, 48:50].bitcast(F32), 1.0).then_inc(const_ready, 1)
                if name == "const_v":
                    step(g.memset(vs[:, :, :, :, 16:32], 0.0))
                    g.memset(vs[:, :, :, :, 16:17], 1.0).then_inc(const_ready, 1)
                if name == "const_sel":
                    step(g.memset(sel_f, 0.0))
                    g.memset(shs1[:, :].bitcast(F32), 0.0)
                    for j in range(2):
                        step(g.affine_select(out=sel_f, in_=sel_f, compare_op=ALU.not_equal,
                                             fill=1.0, base=-H1 * j, pattern=[[-1, H1], [0, P]],
                                             channel_multiplier=1))
                    g.tensor_copy(sel[:, :, :], sel_f).then_inc(const_ready, 1)
                if name == "zeros":
                    g.memset(kstk[:, b, :, :].bitcast(F32), 0.0).then_inc(kzero_ready, 1)
                if name == "mask":
                    pool.wait_ge(s_mask, 16)
                    g.tensor_scalar(mask_add[:, :, :, :], mask_u8, -1.0, -NEG, ALU.add, ALU.mult)\
                     .then_inc(mask_ready, 1)
                if name in ("stats0", "stats1", "stats2"):
                    rstd_of(int(name[-1]), b)
                if name == "square0":
                    t = TB * b + i_
                    pool.wait_ge(*emptied(("qk", t)))
                    if t >= TB:
                        pool.wait_ge(stk_hi, t - TB + 1)
                        pool.wait_ge(stk_lo, t - TB + 1)
                    g.tensor_tensor(qn[:, t % TB, :], qk[:, t % TB, :], qk[:, t % TB, :], ALU.mult)\
                     .then_inc(sq_ready, 1)
                if name == "root0":
                    inverse_root(seed_ready, b, 2 * H0)
                    if b == 0:
                        pool.wait_ge(scales_ready, 1)
                    g.tensor_tensor(rn[:, :, 0:H0], rn[:, :, 0:H0], sm[:, :].unsqueeze(1).to_broadcast([P, TB, H0]),
                                    ALU.mult).then_inc(rn_ready, 1)
                if name == "xbias0":
                    tiles = slice(TB * b, TB * b + TB)
                    pool.wait_ge(*emptied(("gam", b)))
                    pool.wait_ge(xh_ready, norm_no[(0, b)] + 1)
                    if b >= 1:
                        pool.wait_ge(x2b_ready, b)
                    step(g.tensor_tensor(term, gam[:, b, 0:C], row[:, R_PF:R_PF + C], ALU.mult))
                    g.tensor_tensor(xs[:, tiles, :], xs[:, tiles, :], term.unsqueeze(1).to_broadcast([P, TB, C]),
                                    ALU.add).then_inc(xb_ready, 1)
                if name == "xbias1":
                    tiles = slice(TB * b, TB * b + TB)
                    pool.wait_ge(xb_ready, b + 1)
                    step(g.tensor_tensor(term, gam[:, b, C:2 * C], row[:, R_PF + C:R_PF + 2 * C], ALU.mult))
                    pool.wait_ge(x2_ready, b + 1)
                    g.tensor_tensor(xs[:, tiles, :], x2[:, tiles, :], term.unsqueeze(1).to_broadcast([P, TB, C]),
                                    ALU.add).then_inc(x2b_ready, 1)
                if name == "split_w1":
                    pool.wait_ge(w_hi, 3)
                    g.tensor_tensor(w1_lo, stage_a[:, 0:FC * HID].rearrange("p (f n) -> p f n", f=FC),
                                    w1_hi, ALU.subtract).then_inc(w_lo_p, 1)
                if name == "split_w2":
                    pool.wait_ge(w_hi, 4)
                    g.tensor_tensor(w2_lo, stage_b[:, :].rearrange("p (f n) -> p f n", f=HC),
                                    w2_hi, ALU.subtract).then_inc(w_lo_p, 1)
                if name == "split_wqkv1":
                    pool.wait_ge(w_hi, 5)
                    g.tensor_tensor(wqkv_lo[:, :, :], stage_a[:, 0:FC * 3 * C].rearrange("p (f n) -> p f n", f=FC),
                                    wqkv_hi[:, :, :], ALU.subtract).then_inc(w_lo_p, 1)
                if name == "split_wout1":
                    pool.wait_ge(w_hi, 6)
                    g.tensor_tensor(wo_lo[:, :, :], stage_b[:, 0:FC * C].rearrange("p (f n) -> p f n", f=FC),
                                    wo_hi[:, :, :], ALU.subtract).then_inc(w_lo_p, 1)
                if name == "hlo":
                    n = (HC // 2) * b + i_
                    pool.wait_ge(h_hi_ready, n + 1)
                    g.tensor_tensor(h_lo[b % 2][:, 2 * i_:2 * i_ + 2, :],
                                    gelu_u[:, n % 4, :].rearrange("p (a n) -> p a n", a=2),
                                    h_hi[b % 2][:, 2 * i_:2 * i_ + 2, :], ALU.subtract).then_inc(h_lo_ready, 1)
                if name == "square1":
                    t = TB * b + i_
                    pool.wait_ge(*emptied(("qk1", t)))
                    if t >= TB:
                        pool.wait_ge(stk1_hi, t - TB + 1)
                        pool.wait_ge(stk1_lo, t - TB + 1)
                    g.tensor_tensor(qn[:, t % TB, :], qk[:, t % TB, :], qk[:, t % TB, :], ALU.mult)\
                     .then_inc(sq1_ready, 1)
                if name == "root1":
                    inverse_root(seed1_ready, b, 2 * H1)
                    g.tensor_tensor(rn[:, :, 0:2 * H1], rn[:, :, 0:2 * H1],
                                    sqs[:, :].unsqueeze(1).to_broadcast([P, TB, 2 * H1]), ALU.mult).then_inc(rn1_ready, 1)
                if name == "cos":
                    t = TB * b + i_
                    if t == 0:
                        pool.wait_ge(s_rope, 16)
                        pool.wait_ge(w_hi, 5)
                        pool.wait_ge(w_lo_p, 3)
                    pool.wait_ge(*emptied(("qk1", t)))
                    if t >= TB:
                        pool.wait_ge(rope_done, t - TB + 1)
                    g.tensor_tensor(rope_a[:, t % 2, :].rearrange("p (g d) -> p g d", d=D1 // 2),
                                    qk[:, t % TB, :].rearrange("p (g d) -> p g d", d=D1 // 2),
                                    rope_sb[:, t % TB, 0:1, :].to_broadcast([P, 4 * H1, D1 // 2]),
                                    ALU.mult).then_inc(cos_done, 1)
                if name == "head_scales":
                    pool.wait_ge(s_row, 16)
                    g.tensor_tensor(sqs[:, 0:H1], row[:, R_SC:R_SC + H1], half_pos[:, 0:H1], ALU.pow)
                    step(g.tensor_tensor(sqs[:, H1:2 * H1], row[:, R_SC:R_SC + H1], half_pos[:, 0:H1], ALU.pow))

        @block.scalar
        def _(act):
            a = nc.scalar

            def split_hi(s, amount, dst, src):
                act.wait_ge(s, amount)
                a.activation(dst, src, ACT.Copy).then_inc(w_hi, 1)

            def modulate(kind, b):
                key = ("xT", kind, b)
                n = norm_no[(kind, b)]
                act.wait_ge(*full(key))
                if n == 0:
                    act.wait_ge(mod_ready, 1)
                if kind == 1 and b == 0:
                    act.wait_ge(mod_ready, 2)
                if n >= 1:
                    act.wait_ge(xm_ready, n)
                src = bank(key).rearrange("p (f n) -> p f n", f=FC)
                for f in range(FC):
                    if kind == 2:
                        ins = a.activation(xmt[:, f, :], src[:, f, :], ACT.Identity, bias=0.0,
                                           scale=mod[:, 8 + f, b:b + 1])
                    else:
                        ins = a.activation(xmt[:, f, :], src[:, f, :], ACT.Identity,
                                           bias=mod[:, 4 + 2 * kind + f, b:b + 1],
                                           scale=mod[:, 2 * kind + f, b:b + 1])
                ins.then_inc(ring_act, 1)

            def exps(n, free):
                act.wait_ge(s_full, n + 1)
                if free:
                    act.wait_ge(pv_full, free)
                a.activation(ps[:, n % 4], psx[:, n % 2], ACT.Exp).then_inc(exp_done, 1)

            def take_heads(key, read_before):
                act.wait_ge(*full(key))
                act.wait_ge(*full(read_before))
                src = bank(key).rearrange("p (f n) -> p f n", f=FC)
                a.activation(at[:, :, :], src, ACT.Copy)
                a.activation(at_hi[:, :, :], src, ACT.Copy).then_inc(ring_act, 1)

            def take_o(b, u):
                k = 2 * b + u
                act.wait_ge(pv_full, 4 * b + 2 * u + 2)
                if k >= 2:
                    act.wait_ge(*full(("oT", (k - 2) // 2, k % 2)))
                else:
                    act.wait_ge(const_ready, 4)
                    act.wait_ge(flag_ready, 1)
                    act.wait_ge(rows_ready, 1)
                a.activation(o_raw[:, k % 2, :], pv[:, :], ACT.Copy).then_inc(pv_taken, 1)

            for step_ in ORDER:
                name, b = step_[0], step_[1] if len(step_) > 1 else None
                i_ = step_[2] if len(step_) > 2 else None
                if name == "silu":
                    act.wait_ge(s_col, 16)
                    a.activation(silu[:, 0, :], col[:, 0:FC * B], ACT.Exp, scale=-1.0).then_inc(silu_exp, 1)
                if name == "head_scales":
                    act.wait_ge(sml_min, 1)
                    a.activation(sm[:, :], sm[:, :], ACT.Exp).then_inc(scales_ready, 1)
                if name == "split_wqkv0":
                    split_hi(s_wq, 16, wqkv_hi[:, :, :], stage_b[:, 0:FC * 3 * C].rearrange("p (f n) -> p f n", f=FC))
                if name == "split_wproj":
                    split_hi(s_wp, 16, wp_hi[:, :, :], stage_b[:, FC * 3 * C:FC * 4 * C].rearrange("p (f n) -> p f n", f=FC))
                if name in ("normed0", "normed1", "normed2"):
                    modulate(int(name[-1]), b)
                if name == "gamma":
                    act.wait_ge(*full(("gam", b)))
                    if b == 0:
                        act.wait_ge(*full(("ada2",)))
                    a.activation(gam[:, b, :], bank(("gam", b)), ACT.Copy, scale=0.5).then_inc(ring_act, 1)
                if name == "hi0":
                    t = TB * b + i_
                    act.wait_ge(qn_ready, t + 1)
                    if t >= TB:
                        act.wait_ge(*full(("kT", t - TB, 1)))
                    s = stack[:, t % TB]
                    q = qn[:, t % TB, :].rearrange("p (h d) -> p h d", d=D0)
                    a.activation(s[:, :, 0:16], q, ACT.Copy).then_inc(stk_hi_first, 1)
                    a.activation(s[:, 0:H0, 16:32], q[:, 0:H0], ACT.Copy)
                    a.activation(s[:, H0:2 * H0, 32:48], q[:, H0:2 * H0], ACT.Copy).then_inc(stk_hi, 1)
                if name == "turnq0":
                    t = TB * b + i_
                    if i_ == 0 and b >= 2:
                        act.wait_ge(s_full, PAIRS * (b - 1))
                    for u in range(2):
                        key = ("qT", t, u)
                        act.wait_ge(*full(key))
                        a.activation(qstk[:, b % 2, 4 * u:4 * u + 4, i_ * P:i_ * P + P],
                                     bank(key).rearrange("p (a n) -> p a n", a=4), ACT.Copy).then_inc(ring_act, 1)
                if name == "turnk0":
                    t = TB * b + i_
                    if i_ == 0 and b < 2:
                        act.wait_ge(kzero_ready, b + 1)
                    if i_ == 0 and b >= 2:
                        act.wait_ge(s_full, PAIRS * (b - 1))
                    for u in range(2):
                        key = ("kT", t, u)
                        act.wait_ge(*full(key))
                        src = bank(key).rearrange("p (a n) -> p a n", a=4)
                        dst = kstk[:, b % 2, :, i_ * P:i_ * P + P].rearrange("p (a c) n -> p a c n", c=2)[:, 4 * u:4 * u + 4]
                        a.activation(dst[0:SLOT, :, 0, :], src[0:SLOT], ACT.Copy)
                        a.activation(dst[SLOT:P, :, 1, :], src[SLOT:P], ACT.Copy).then_inc(ring_act, 1)
                if name == "score0":
                    n = PAIRS * b + i_
                    exps(n, (n - 4) // 2 + 1 if n >= 4 else 0)
                if name == "take0":
                    take_o(b, i_)
                if name == "heads0":
                    take_heads(("aT", b), ("pj", b - 1) if b >= 1 else ("gam", B - 1))
                if name == "split_w1":
                    act.wait_ge(s_full, 3 * PAIRS)
                    split_hi(s_w1, 16, w1_hi, stage_a[:, 0:FC * HID].rearrange("p (f n) -> p f n", f=FC))
                if name == "split_w2":
                    act.wait_ge(s_full, 4 * PAIRS)
                    split_hi(s_w2, 16, w2_hi, stage_b[:, :].rearrange("p (f n) -> p f n", f=HC))
                if name == "split_wqkv1":
                    act.wait_ge(*full(("v", B - 1)))
                    split_hi(s_wq1, 16, wqkv_hi[:, :, :], stage_a[:, 0:FC * 3 * C].rearrange("p (f n) -> p f n", f=FC))
                if name == "split_wout1":
                    split_hi(s_wo, 16, wo_hi[:, :, :], stage_b[:, 0:FC * C].rearrange("p (f n) -> p f n", f=FC))
                if name == "fc1":
                    n = (HC // 2) * b + i_
                    key = ("f1", b, i_)
                    if n == 0:
                        act.wait_ge(pv_full, 4 * B)
                    act.wait_ge(*full(key))
                    if n >= 4:
                        act.wait_ge(h_lo_ready, n - 3)
                    for i in range(2):
                        last = a.activation(gelu_u[:, n % 4, i * L:(i + 1) * L], bank(key)[:, i * L:(i + 1) * L],
                                            ACT.Identity, bias=col[:, 16 + 2 * i_ + i:17 + 2 * i_ + i])
                    last.then_inc(ring_act, 1)
                    act.wait_ge(*emptied(key))
                    a.activation(gelu_z[:, n % 4, :], gelu_u[:, n % 4, :], ACT.Square).then_inc(sq_u, 1)
                if name == "tanh":
                    n = (HC // 2) * b + i_
                    act.wait_ge(z_ready, n + 1)
                    a.activation(gelu_z[:, n % 4, :], gelu_z[:, n % 4, :], ACT.Tanh, scale=GELU_C * GELU_A)\
                     .then_inc(t_ready, 1)
                if name == "qk1":
                    t = TB * b + i_
                    act.wait_ge(*full(("qk1", t)))
                    if t < TB:
                        act.wait_ge(qn_ready, NT)
                    else:
                        act.wait_ge(cos_done, t - TB + 1)
                        act.wait_ge(rope_done, t - TB + 1)
                    a.activation(qk[:, t % TB, :], bank(("qk1", t)), ACT.Copy).then_inc(ring_act, 1)
                if name == "v1":
                    act.wait_ge(*full(("v1", b)))
                    if b >= 3:
                        act.wait_ge(pv_full, 16 + 2 * (b - 3) + 2)
                    a.activation(v1[:, b % 3, :, :], bank(("v1", b)).rearrange("p (t n) -> p t n", t=TB), ACT.Copy)\
                     .then_inc(ring_act, 1)
                if name == "hi1":
                    t = TB * b + i_
                    act.wait_ge(rope_done, t + 1)
                    act.wait_ge(*full(("k1T1", t - TB) if t >= TB else ("f2", B - 1)))
                    s = stk1[:, t % TB]
                    r = qn[:, t % TB, :].rearrange("p (h d) -> p h d", d=D1)
                    a.activation(s[:, 0:H1, 0:D1], r[:, 0:H1], ACT.Copy)
                    a.activation(s[:, H1:2 * H1, 0:D1], r[:, H1:2 * H1], ACT.Copy).then_inc(stk1_hi_first, 1)
                    a.activation(s[:, H1:2 * H1, D1:2 * D1], r[:, H1:2 * H1], ACT.Copy).then_inc(stk1_hi, 1)
                if name == "turn1":
                    t = TB * b + i_
                    tok = slice(i_ * P, i_ * P + P)
                    if i_ == 0:
                        act.wait_ge(*full(("f2", B - 1)))
                        if b >= 2:
                            act.wait_ge(s_full, PAIRS * B + 2 * (b - 1))
                    for i, w in enumerate(("q1T", "k1T0", "k1T1")):
                        act.wait_ge(*full((w, t)))
                        dst = q1[:, b % 2, :, tok] if i == 0 else k1[:, b % 2, i - 1, :, tok]
                        a.activation(dst, bank((w, t)).rearrange("p (a n) -> p a n", a=4), ACT.Copy)\
                         .then_inc(ring_act, 1)
                if name == "score1":
                    n = PAIRS * B + 2 * b + i_
                    if n == PAIRS * B:
                        act.wait_ge(h_lo_ready, B * HC // 2)
                    exps(n, 4 * B + 2 * (b - 2) + 2 if b >= 2 else 4 * B)
                if name == "sum1":
                    act.wait_ge(pv_full, 16 + 2 * b + 1)
                    if b == 0:
                        act.wait_ge(*full(("oT", B - 1, 1)))
                    else:
                        act.wait_ge(*full(("sT1", b - 1)))
                    a.activation(o_raw[:, 0, 0:L], pv[:, 0:L], ACT.Copy).then_inc(pv_taken, 1)
                if name == "value1":
                    act.wait_ge(pv_full, 16 + 2 * b + 2)
                    if b >= 1:
                        act.wait_ge(*full(("oT1", b - 1)))
                    a.activation(o_raw[:, 1, :], pv[:, :], ACT.Copy).then_inc(pv_taken, 1)
                if name == "heads1":
                    take_heads(("aT1", b), ("pj", B - 1) if b == 0 else ("po", b - 1))

        @block.tensor
        def _(pe):
            mm = nc.tensor.matmul

            def claim(key):
                before = previous_in_bank(key)
                if before is not None:
                    pe.wait_ge(*emptied(before))
                return bank(key)

            def three(dst, lhs, rhs, start, stop):
                mm(dst, lhs[0], rhs[0], start=start, stop=False)
                mm(dst, lhs[0], rhs[1], start=False, stop=False)
                return mm(dst, lhs[1], rhs[0], start=False, stop=stop)

            def transposes(dst, sources, idt=None):
                for i, src in enumerate(sources):
                    last = nc.tensor.transpose(dst[:, i * P:(i + 1) * P], src, ident[:, :])
                return last

            def adaptive(dst, chunks):
                for j in chunks:
                    for f in range(FC):
                        last = mm(dst[:, B * j:B * j + B], wada_sb[:, f, 2 * C + j * P:2 * C + (j + 1) * P],
                                  silu[:, 2, f * B:(f + 1) * B], start=(f == 0), stop=(f == FC - 1))
                return last

            def norm_transposed(kind, b):
                key = ("xT", kind, b)
                dst = claim(key)
                pe.wait_ge(xh_ready, norm_no[(kind, b)] + 1)
                transposes(dst, [xh[:, t, f * P:(f + 1) * P] for f in range(FC) for t in range(TB)])\
                    .then_inc(ring_full, 1)

            def operand(kind, b, f, tok):
                s = norm_no[(kind, b)] % 2
                return xm_hi[:, s, f, tok], xm_lo[:, s, f, tok]

            def qk_products(kind, b, i, key):
                pe.wait_ge(xm_ready, norm_no[(kind, b)] + 1)
                dst = claim(key)
                for f in range(FC):
                    last = three(dst, operand(kind, b, f, slice(i * P, i * P + P)),
                                 (wqkv_hi[:, f, 0:2 * C], wqkv_lo[:, f, 0:2 * C]), f == 0, f == FC - 1)
                last.then_inc(ring_full, 1)

            def v_products(kind, b, key):
                dst = claim(key)
                pe.wait_ge(xm_ready, norm_no[(kind, b)] + 1)
                for i in range(TB):
                    tok = slice(i * P, i * P + P)
                    for f in range(FC):
                        last = three(dst[:, i * C:(i + 1) * C], operand(kind, b, f, tok),
                                     (wqkv_hi[:, f, 2 * C:3 * C], wqkv_lo[:, f, 2 * C:3 * C]), f == 0, f == FC - 1)
                last.then_inc(ring_full, 1)

            def max_scores(b, qc, p, with_bias):
                key = ("mx", b, qc, p)
                dst = claim(key)
                if (qc, p) == (0, 0):
                    for w in ("qT", "kT"):
                        pe.wait_ge(*emptied((w, TB * b + 1, 1)))
                last = mm(dst, qstk[:, b % 2, p, qc * P:(qc + 1) * P], kstk[:, b % 2, 2 * p:2 * p + 2, :],
                          start=True, stop=not with_bias)
                if with_bias:
                    for i in range(2):
                        last = mm(dst[:, i * L:(i + 1) * L], ident[:, :], bias_sb[:, qc, :], start=False, stop=(i == 1))
                last.then_inc(ring_full, 1)

            def shift_transposed(b):
                dst = claim(("shT", b))
                pe.wait_ge(shp_ready, b + 1)
                for qc in range(TB):
                    last = nc.tensor.transpose(dst[0:4 * PAIRS, qc * P:(qc + 1) * P],
                                               shp[:, qc, :, :, :].rearrange("p a j h -> p (a j h)"), ident[:, :])
                last.then_inc(ring_full, 1)

            def key_major_scores(b, p, with_bias):
                n = PAIRS * b + p
                if n >= 2:
                    pe.wait_ge(exp_done, n - 1)
                if p == 0:
                    pe.wait_ge(shift_in, 32 * (b + 1))
                dst = psx[:, n % 2]
                for i in range(2):
                    for kc in range(TB):
                        keys = slice(kc * P, kc * P + P)
                        last = mm(dst[:, i, kc, :], kstk[:, b % 2, 2 * p + i, keys], qstk[:, b % 2, p, :],
                                  start=True, stop=not with_bias)
                        if with_bias:
                            for qc in range(TB):
                                last = mm(dst[:, i, kc, qc * P:(qc + 1) * P], bias_sb[:, qc, keys], ident[:, :],
                                          start=False, stop=(qc == TB - 1))
                last.then_inc(s_full, 1)

            def weighted_values(b, g):
                if g % 2 == 0 and (b or g):
                    pe.wait_ge(pv_taken, 2 * b + g // 2)
                pe.wait_ge(exp_done, PAIRS * b + 2 * g + 2)
                if g == 0:
                    pe.wait_ge(*emptied(("v", b)))
                    pe.wait_ge(const_ready, 3)
                cols_ = slice((g % 2) * L, (g % 2) * L + L)
                for kc in range(TB):
                    for i in range(4):
                        slot = (PAIRS * b + 2 * g + i // 2) % 4
                        last = mm(pv[32 * i:32 * i + 32, cols_], vs[:, b % 3, kc, 4 * g + i, :],
                                  ps[:, slot, i % 2, kc, :], start=(kc == 0), stop=(kc == TB - 1))
                last.then_inc(pv_full, 1)

            def output_token_major(b, u):
                key = ("oT", b, u)
                dst = claim(key)
                pe.wait_ge(pv_taken, 2 * b + u + 1)
                k = 2 * b + u
                transposes(dst, [o_raw[:, k % 2, i * P:(i + 1) * P] for i in range(4)]).then_inc(ring_full, 1)

            def heads_transposed(b, key, source):
                dst = claim(key)
                pe.wait_ge(*emptied(source))
                transposes(dst, [o_tok[:, t, f * P:(f + 1) * P] for f in range(FC) for t in range(TB)])\
                    .then_inc(ring_full, 1)

            def project(key, n, w):
                dst = claim(key)
                pe.wait_ge(at_ready, n + 1)
                for i in range(TB):
                    tok = slice(i * P, i * P + P)
                    for f in range(FC):
                        last = three(dst[:, i * C:(i + 1) * C], (at_hi[:, f, tok], at_lo[:, f, tok]),
                                     (w[0][:, f, :], w[1][:, f, :]), f == 0, f == FC - 1)
                last.then_inc(ring_full, 1)

            def walk(steps, with_bias):
                for step_ in steps:
                    name, b = step_[0], step_[1] if len(step_) > 1 else None
                    i_ = step_[2] if len(step_) > 2 else None
                    if name == "ada":
                        pe.wait_ge(const_ready, 1)
                        pe.wait_ge(s_wada, 32)
                        pe.wait_ge(silu_ready, 1)
                        adaptive(claim(("ada",)), (0, 1, 4, 5)).then_inc(ring_full, 1)
                    if name == "ada_rest":
                        pe.wait_ge(s_wada2, 48)
                        pe.wait_ge(s_norm, 16)
                        dst = claim(("ada2",))
                        adaptive(dst, (2, 3, 6, 7))
                        for j in range(FC):
                            for f in range(FC):
                                last = mm(dst[:, B * (8 + j):B * (9 + j)], wnorm_sb[:, f, j * P:(j + 1) * P],
                                          col[:, f * B:(f + 1) * B], start=(f == 0), stop=(f == FC - 1))
                        last.then_inc(ring_full, 1)
                    if name == "flag":
                        dst = claim(("flag",))
                        pe.wait_ge(flag_ready, 1)
                        mm(dst[0:1, 0:1], cnt[:, :], ones[:, 0:1], start=True, stop=True).then_inc(ring_full, 1)
                    if name == "gamma_rows":
                        pe.wait_ge(silu2_ready, 1)
                        pe.wait_ge(s_wada2, 48)
                        dst = claim(("gam_rows",))
                        for f in range(FC):
                            last = mm(dst[0:2 * B, :], silu2[:, f, :], wada_sb[:, f, 0:2 * C], start=(f == 0),
                                      stop=(f == FC - 1))
                        last.then_inc(ring_full, 1)
                    if name == "gamma":
                        pe.wait_ge(rows_ready, 1)
                        if b == 0:
                            pe.wait_ge(const_ready, 4)
                        dst = claim(("gam", b))
                        for part, stop in ((at_hi, False), (at_lo, True)):
                            last = mm(dst, sel[0:2 * B, b, :], part[0:2 * B, :, :].rearrange("p f n -> p (f n)"),
                                      start=not stop, stop=stop)
                        last.then_inc(ring_full, 1)
                    if name in ("normed0", "normed1", "normed2"):
                        norm_transposed(int(name[-1]), b)
                    if name == "qk0":
                        if b == 0 and i_ == 0:
                            pe.wait_ge(w_lo_d, 1)
                        qk_products(0, b, i_, ("qk", TB * b + i_))
                    if name == "v0":
                        v_products(0, b, ("v", b))
                    if name in ("turnq0", "turnk0"):
                        t = TB * b + i_
                        if t == 0:
                            pe.wait_ge(const_ready, 2)
                        pe.wait_ge(stk_hi, t + 1)
                        pe.wait_ge(stk_lo, t + 1)
                        flat = stack_flat[:, t % TB].bitcast(F32)
                        base = H0 * SLOT if name == "turnk0" else 0
                        for u in range(2):
                            dst = claim((name[4] + "T", t, u))
                            transposes(dst, [flat[:, base + (4 * u + i) * P:base + (4 * u + i + 1) * P]
                                             for i in range(4)]).then_inc(ring_full, 1)
                    if name == "max0":
                        for q in (2 * i_, 2 * i_ + 1):
                            max_scores(b, q // PAIRS, q % PAIRS, with_bias)
                    if name == "shift0":
                        shift_transposed(b)
                    if name == "score0":
                        key_major_scores(b, i_, with_bias)
                    if name == "value0":
                        weighted_values(b, i_)
                    if name == "out0":
                        output_token_major(b, i_)
                    if name == "heads0":
                        heads_transposed(b, ("aT", b), ("oT", b, 1))
                    if name == "proj0":
                        if b == 0:
                            pe.wait_ge(w_lo_d, 2)
                        project(("pj", b), b, (wp_hi, wp_lo))
                    if name == "fc1":
                        if i_ == 0:
                            pe.wait_ge(xm_ready, norm_no[(1, b)] + 1)
                        if b == 0 and i_ == 0:
                            pe.wait_ge(w_lo_p, 1)
                        dst = claim(("f1", b, i_))
                        for i in range(2):
                            c = slice((2 * i_ + i) * P, (2 * i_ + i + 1) * P)
                            for f in range(FC):
                                last = three(dst[:, i * L:(i + 1) * L], (w1_hi[:, f, c], w1_lo[:, f, c]),
                                             operand(1, b, f, slice(0, L)), f == 0, f == FC - 1)
                        last.then_inc(ring_full, 1)
                    if name == "fc2":
                        if b == 0:
                            pe.wait_ge(w_lo_p, 2)
                        dst = claim(("f2", b))
                        pe.wait_ge(h_lo_ready, (HC // 2) * (b + 1))
                        for i in range(TB):
                            tok = slice(i * P, i * P + P)
                            for c in range(HC):
                                last = three(dst[:, i * C:(i + 1) * C], (h_hi[b % 2][:, c, tok], h_lo[b % 2][:, c, tok]),
                                             (w2_hi[:, c, :], w2_lo[:, c, :]), c == 0, c == HC - 1)
                        last.then_inc(ring_full, 1)
                    if name == "qk1":
                        if b == 0 and i_ == 0:
                            pe.wait_ge(w_lo_p, 3)
                        qk_products(2, b, i_, ("qk1", TB * b + i_))
                    if name == "v1":
                        v_products(2, b, ("v1", b))
                    if name == "turn1":
                        t = TB * b + i_
                        pe.wait_ge(stk1_hi, t + 1)
                        pe.wait_ge(stk1_lo, t + 1)
                        for i, w in enumerate(("q1T", "k1T0", "k1T1")):
                            dst = claim((w, t))
                            transposes(dst, [stk1[:, t % TB, 4 * i + h, :].bitcast(F32) for h in range(H1)])\
                                .then_inc(ring_full, 1)
                    if name == "max1":
                        for hp in range(2):
                            dst = claim(("mx1", b, i_, hp))
                            if (i_, hp) == (0, 0):
                                pe.wait_ge(*emptied(("k1T1", TB * b + 1)))
                            for i in range(2):
                                h = 2 * hp + i
                                for w in range(2):
                                    mm(dst[:, i * L:(i + 1) * L], q1[:, b % 2, h, i_ * P:(i_ + 1) * P],
                                       k1[:, b % 2, w, h, :], start=(w == 0), stop=False)
                                last = mm(dst[:, i * L:(i + 1) * L], ident_b[:, :], mask_add[:, b, i_, :],
                                          start=False, stop=True)
                            last.then_inc(ring_full, 1)
                    if name == "shift1":
                        dst = claim(("shT1", b))
                        pe.wait_ge(sh1_ready, b + 1)
                        for qc in range(TB):
                            last = nc.tensor.transpose(dst[0:2 * H1, qc * P:(qc + 1) * P], sh1[:, qc, :], ident[:, :])
                        last.then_inc(ring_full, 1)
                    if name == "score1":
                        n = PAIRS * B + 2 * b + i_
                        pe.wait_ge(exp_done, n - 1)
                        if i_ == 0:
                            pe.wait_ge(*emptied(("shT1", b)))
                            pe.wait_ge(const_ready, 4)
                        for i in range(2):
                            h = 2 * i_ + i
                            for kc in range(TB):
                                keys = slice(kc * P, kc * P + P)
                                dst = psx[:, n % 2, i, kc, :]
                                for w in range(2):
                                    mm(dst, k1[:, b % 2, w, h, keys], q1[:, b % 2, h, :],
                                       start=(w == 0), stop=False)
                                for qc in range(TB):
                                    mm(dst[:, qc * P:(qc + 1) * P], mask_add[:, b, qc, keys], ident_b[:, :],
                                       start=False, stop=False)
                                last = mm(dst, sel[:, h, :], shs1[:, :], start=False, stop=True)
                        last.then_inc(s_full, 1)
                    if name == "sum1":
                        first = PAIRS * B + 2 * b
                        pe.wait_ge(pv_taken, 2 * B + 2 * b)
                        pe.wait_ge(exp_done, first + 2)
                        for kc in range(TB):
                            for h in range(H1):
                                last = mm(pv[32 * h:32 * h + 32, 0:L], ones[:, :], ps[:, (first + h // 2) % 4, h % 2, kc, :],
                                          start=(kc == 0), stop=(kc == TB - 1))
                        last.then_inc(pv_full, 1)
                    if name == "value1":
                        first = PAIRS * B + 2 * b
                        pe.wait_ge(pv_taken, 2 * B + 2 * b + 1)
                        for hp in range(2):
                            for kc in range(TB):
                                for i in range(2):
                                    h = 2 * hp + i
                                    last = mm(pv[64 * i:64 * i + 64, hp * L:(hp + 1) * L],
                                              v1[:, b % 3, kc, h * D1:(h + 1) * D1],
                                              ps[:, (first + hp) % 4, i, kc, :], start=(kc == 0), stop=(kc == TB - 1))
                        last.then_inc(pv_full, 1)
                    if name == "out1":
                        dst = claim(("sT1", b))
                        transposes(dst, [o_raw[:, 0, qc * P:(qc + 1) * P] for qc in range(TB)]).then_inc(ring_full, 1)
                        dst = claim(("oT1", b))
                        pe.wait_ge(pv_taken, 2 * B + 2 * b + 2)
                        transposes(dst, [o_raw[:, 1, i * P:(i + 1) * P] for i in range(4)]).then_inc(ring_full, 1)
                    if name == "heads1":
                        heads_transposed(b, ("aT1", b), ("oT1", b))
                    if name == "proj1":
                        if b == 0:
                            pe.wait_ge(w_lo_p, 4)
                        project(("po", b), B + b, (wo_hi, wo_lo))

            walk(ORDER[:FIRST_SCORE], False)
            pe.wait_ge(*emptied(("flag",)))
            bias_flag = nc.tensor.value_load(flag[0:1, 0:1], min_val=0, max_val=1 << 20)
            with nc.tensor.If(bias_flag == 0):
                walk(ORDER[FIRST_SCORE:AFTER_SCORES], False)
            with nc.tensor.If(bias_flag != 0):
                walk(ORDER[FIRST_SCORE:AFTER_SCORES], True)
            walk(ORDER[AFTER_SCORES:], False)

        @block.vector
        def _(dve):
            v = nc.vector
            step = stepper(dve, dve_step)

            def adaptive(key, firsts, with_norm):
                dve.wait_ge(*full(key))
                src = bank(key)[:, 0:10 * B].rearrange("p (j n) -> p j n", n=B)
                for j in firsts:
                    last = v.tensor_tensor(mod[:, j:j + 2, :], src[:, j:j + 2, :],
                                           col[:, 8 + j:10 + j].unsqueeze(2).to_broadcast([P, 2, B]), ALU.add)
                    if j < 4:
                        step(last)
                if with_norm:
                    last = v.tensor_scalar(mod[:, 8:10, :], src[:, 8:10, :], 1.0, None, ALU.add)
                last.then_inc(ring_dve, 1)
                dve.wait_ge(*emptied(key))
                v.tensor_scalar(mod[:, firsts[0]:firsts[0] + 2, :], mod[:, firsts[0]:firsts[0] + 2, :], 1.0, None,
                                ALU.add).then_inc(mod_ready, 1)

            def split_lo(n, hi, lo, src):
                dve.wait_ge(w_hi, n)
                v.tensor_tensor(lo[:, :, :], src.rearrange("p (f n) -> p f n", f=FC), hi[:, :, :], ALU.subtract)\
                 .then_inc(w_lo_d, 1)

            def seed(b, n, least, seeded):
                y, x_, t = rn[:, :, 0:n], ss[:, :, 0:n], nt[:, :, 0:n]
                step(least)
                step(v.tensor_scalar(t.bitcast(I32), x_.bitcast(I32), 1, None, ALU.logical_shift_right))
                v.tensor_scalar(y.bitcast(I32), t.bitcast(I32), -1.0, float(0x5f3759df), ALU.mult, ALU.add)\
                 .then_inc(seeded, 1)

            def statistics(kind, b, src):
                for i in range(TB):
                    step(v.bn_stats(bnst[:, kind, b, i, :], src[:, TB * b + i, :]))
                for i in range(TB):
                    step(v.bn_aggr(mv[:, kind, b, i, :], bnst[:, kind, b, i, :]))
                if kind < 2:
                    v.tensor_scalar(ve[:, kind, b, :], mv[:, kind, b, :, 1], LN_EPS, None, ALU.add).then_inc(stats_ready, 1)
                else:
                    step(v.tensor_tensor(ve[:, kind, b, :], mv[:, kind, b, :, 0], mv[:, kind, b, :, 0], ALU.mult))
                    v.scalar_tensor_tensor(ve[:, kind, b, :], ve[:, kind, b, :], LN_EPS, mv[:, kind, b, :, 1],
                                           ALU.add, ALU.add).then_inc(stats_ready, 1)

            def normalise(kind, b, src):
                n = norm_no[(kind, b)]
                dve.wait_ge(rstd_ready, stat_no[(kind, b)] + 1)
                if n >= 1:
                    dve.wait_ge(*full(("xT",) + norm_keys[n - 1]))
                for i in range(TB):
                    mean = mv[:, kind, b, i, 0:1] if kind < 2 else zero_col[:, :]
                    ins = v.tensor_scalar(xh[:, i, :], src[:, TB * b + i, :], mean, rstd[:, kind, b, i:i + 1],
                                          ALU.subtract, ALU.mult)
                ins.then_inc(xh_ready, 1)

            def split_norm(kind, b):
                n = norm_no[(kind, b)]
                dve.wait_ge(*emptied(("xT", kind, b)))
                if n >= 2:
                    dve.wait_ge(*full(last_matmul_of_norm(*norm_keys[n - 2])))
                step(v.tensor_copy(xm_hi[:, n % 2], xmt[:, :, :]))
                v.tensor_tensor(xm_lo[:, n % 2], xmt[:, :, :], xm_hi[:, n % 2], ALU.subtract).then_inc(xm_ready, 1)

            def row_max(b, qc, p):
                key = ("mx", b, qc, p)
                if b >= 1 and (qc, p) == (0, 0):
                    dve.wait_ge(shp_ready, b)
                dve.wait_ge(*full(key))
                v.tensor_reduce(nm[:, qc, :, p], bank(key).rearrange("p (h n) -> p h n", h=2), AX.X, ALU.max,
                                negate=True).then_inc(ring_dve, 1)

            def token_major_output(b, u):
                key = ("oT", b, u)
                dve.wait_ge(*full(key))
                src = bank(key).rearrange("p (q i s) -> p q i s", q=4, i=4)
                if 2 * b + u >= 1:
                    dve.wait_ge(*emptied(("oT", (2 * b + u - 1) // 2, (u + 1) % 2)))
                step(v.reciprocal(rv[:, :, :], src[:, :, :, D0]))
                if u == 0 and b == 0:
                    dve.wait_ge(mask_ready, 1)
                if u == 0 and b >= 1:
                    dve.wait_ge(*full(("aT", b - 1)))
                ot = o_tok[:, :, :].rearrange("p t (h d) -> p t h d", d=D0)
                for half in range(2):
                    h = 8 * u + 4 * half
                    ins = v.tensor_tensor(ot[:, :, h:h + 4, :], src[:, 2 * half:2 * half + 2, :, 0:D0],
                                          rv[:, 2 * half:2 * half + 2, :].unsqueeze(3).to_broadcast([P, TB, 4, D0]),
                                          ALU.mult)
                ins.then_inc(ring_dve, 1)

            def negative_max(m):
                dve.wait_ge(*emptied(("mx", m, TB - 1, PAIRS - 1)))
                if m >= 1:
                    dve.wait_ge(*full(("shT", m - 1)))
                step(v.tensor_copy(shp[:, :, :, 0, :].bitcast(F32R), nm[:, :, :, :]))
                v.tensor_tensor(shp[:, :, :, 1, :].bitcast(F32R), nm[:, :, :, :], shp[:, :, :, 0, :], ALU.subtract)\
                 .then_inc(shp_ready, 1)

            def shift_rows(m):
                dve.wait_ge(*full(("shT", m)))
                if m >= 1:
                    dve.wait_ge(shift_in, 32 * m)
                v.tensor_copy(shs, bank(("shT", m))[0:4 * PAIRS, 0:L]).then_inc(ring_dve, 1)

            def split_heads(key):
                dve.wait_ge(*emptied(key))
                v.tensor_tensor(at_lo[:, :, :], at[:, :, :], at_hi[:, :, :], ALU.subtract)\
                 .then_inc(at_ready, 1)

            for step_ in ORDER:
                name, b = step_[0], step_[1] if len(step_) > 1 else None
                i_ = step_[2] if len(step_) > 2 else None
                tiles = [TB * b + i for i in range(TB)] if b is not None else []
                if name == "silu":
                    dve.wait_ge(silu_exp, 1)
                    step(v.tensor_scalar(silu[:, 1, :], silu[:, 0, :], 1.0, None, ALU.add))
                    step(v.reciprocal(silu[:, 0, :], silu[:, 1, :]))
                    v.tensor_tensor(silu[:, 2, :], silu[:, 0, :], col[:, 0:FC * B], ALU.mult).then_inc(silu_ready, 1)
                    dve.wait_ge(silu_ready, 1)
                    v.tensor_copy(silu2[:, :, :].rearrange("p f (r b) -> p f r b", r=2),
                                  silu[:, 2, :].rearrange("p (f b) -> p f b", f=FC).unsqueeze(2)
                                  .to_broadcast([P, FC, 2, B]))\
                     .then_inc(silu2_ready, 1)
                if name == "head_scales":
                    dve.wait_ge(s_row, 16)
                    v.tensor_scalar(sm[:, :], row[:, R_SML:R_SML + H0], LOG100, None, ALU.min).then_inc(sml_min, 1)
                if name == "ada":
                    adaptive(("ada",), (0, 4), False)
                if name == "split_wqkv0":
                    split_lo(1, wqkv_hi, wqkv_lo, stage_b[:, 0:FC * 3 * C])
                if name == "split_wproj":
                    split_lo(2, wp_hi, wp_lo, stage_b[:, FC * 3 * C:FC * 4 * C])
                if name == "bias_count":
                    dve.wait_ge(s_bias, 16)
                    step(v.tensor_scalar(bias_sb[:, :, :], bias_sb[:, :, :], -3.0e38, None, ALU.max))
                    v.tensor_scalar(o_raw[:, 0, :], bias_sb[:, :, :].rearrange("p t n -> p (t n)"), 0.0, None,
                                    ALU.not_equal, ALU.add, accum_out=cnt[:, :]).then_inc(flag_ready, 1)
                if name == "ada_rest":
                    adaptive(("ada2",), (2, 6), True)
                if name == "flag":
                    dve.wait_ge(*full(("flag",)))
                    v.tensor_copy(flag[:, :], bank(("flag",))[0:1, 0:1]).then_inc(ring_dve, 1)
                if name == "gamma_rows":
                    dve.wait_ge(s_row, 16)
                    dve.wait_ge(flag_ready, 1)
                    dve.wait_ge(*full(("gam_rows",)))
                    v.tensor_tensor(gam_rows, bank(("gam_rows",))[0:2 * B, :], row[0:2 * B, R_GAM:R_GAM + 2 * C], ALU.add)\
                     .then_inc(ring_dve, 1)
                    dve.wait_ge(*emptied(("gam_rows",)))
                    hi, lo = (part[0:2 * B, :, :].rearrange("p f n -> p (f n)") for part in (at_hi, at_lo))
                    v.tensor_copy(hi, gam_rows).then_inc(rows_hi, 1)
                    dve.wait_ge(rows_hi, 1)
                    v.tensor_tensor(lo, gam_rows, hi, ALU.subtract).then_inc(rows_ready, 1)
                if name == "stats0":
                    dve.wait_ge(s_x[b], 16)
                    statistics(0, b, xs)
                if name in ("norm0", "norm1", "norm2"):
                    normalise(int(name[-1]), b, x2 if name == "norm1" else xs)
                if name in ("split0", "split1", "split2"):
                    split_norm(int(name[-1]), b)
                if name == "qk0":
                    t = TB * b + i_
                    dve.wait_ge(*full(("qk", t)))
                    if t == 0:
                        dve.wait_ge(s_row, 16)
                    if t >= TB:
                        dve.wait_ge(qn_ready, t - TB + 1)
                    v.tensor_tensor(qk[:, t % TB, :], bank(("qk", t)), row[:, R_QK:R_QK + 2 * C], ALU.add)\
                     .then_inc(ring_dve, 1)
                if name == "v0":
                    dve.wait_ge(*full(("v", b)))
                    if b >= 3:
                        dve.wait_ge(pv_full, 4 * (b - 2))
                    if b == 0:
                        dve.wait_ge(const_ready, 3)
                    for i in range(TB):
                        ins = v.tensor_tensor(vs[:, b % 3, i, :, 0:D0],
                                              bank(("v", b))[:, i * C:(i + 1) * C].rearrange("p (a d) -> p a d", d=D0),
                                              row[:, R_V:R_V + C].rearrange("p (a d) -> p a d", d=D0), ALU.add)
                    ins.then_inc(ring_dve, 1)
                if name == "sums0":
                    if b >= 1:
                        dve.wait_ge(rn_ready, b)
                    for t in tiles:
                        dve.wait_ge(sq_ready, t + 1)
                        step(v.tensor_reduce(ss[:, t % TB, :], qn[:, t % TB, :].rearrange("p (h d) -> p h d", d=D0),
                                             AX.X, ALU.add))
                    if b >= 1:
                        dve.wait_ge(qn_ready, TB * b)
                    seed(b, 2 * H0, v.tensor_scalar(ss[:, :, :], ss[:, :, :], 1e-24, None, ALU.max), seed_ready)
                if name == "unit0":
                    t = TB * b + i_
                    dve.wait_ge(rn_ready, b + 1)
                    v.tensor_tensor(qn[:, t % TB, :].rearrange("p (h d) -> p h d", d=D0),
                                    qk[:, t % TB, :].rearrange("p (h d) -> p h d", d=D0),
                                    rn[:, t % TB, :].unsqueeze(2).to_broadcast([P, 2 * H0, D0]), ALU.mult)\
                     .then_inc(qn_ready, 1)
                if name == "lo0":
                    t = TB * b + i_
                    dve.wait_ge(stk_hi_first, t + 1)
                    sr = stack[:, t % TB]
                    s = sr.bitcast(F32)
                    q = qn[:, t % TB, :].rearrange("p (h d) -> p h d", d=D0)
                    v.tensor_tensor(sr[:, 0:H0, 32:48], q[:, 0:H0], s[:, 0:H0, 0:16], ALU.subtract)
                    v.tensor_tensor(sr[:, H0:2 * H0, 16:32], q[:, H0:2 * H0], s[:, H0:2 * H0, 0:16], ALU.subtract)\
                     .then_inc(stk_lo, 1)
                if name == "max0":
                    for q in (2 * i_, 2 * i_ + 1):
                        row_max(b, q // PAIRS, q % PAIRS)
                if name == "neg0":
                    negative_max(b)
                if name == "shift0":
                    shift_rows(b)
                if name == "out0":
                    token_major_output(b, i_)
                if name == "heads0_lo":
                    split_heads(("aT", b))
                if name == "proj0":
                    dve.wait_ge(*emptied(("gam", b)))
                    dve.wait_ge(*full(("pj", b)))
                    gam1 = gam[:, b, 0:C].unsqueeze(1).to_broadcast([P, TB, C])
                    batch = slice(TB * b, TB * b + TB)
                    v.tensor_tensor(x2[:, batch, :], bank(("pj", b)).rearrange("p (t n) -> p t n", t=TB), gam1, ALU.mult)\
                     .then_inc(ring_dve, 1)
                    dve.wait_ge(*emptied(("pj", b)))
                    dve.wait_ge(xb_ready, b + 1)
                    v.tensor_tensor(x2[:, batch, :], x2[:, batch, :], xs[:, batch, :], ALU.add).then_inc(x2_ready, 1)
                if name == "stats1":
                    dve.wait_ge(x2_ready, b + 1)
                    statistics(1, b, x2)
                if name == "poly":
                    n = (HC // 2) * b + i_
                    dve.wait_ge(sq_u, n + 1)
                    v.scalar_tensor_tensor(gelu_z[:, n % 4, :], gelu_z[:, n % 4, :], 1.0 / GELU_A,
                                           gelu_u[:, n % 4, :], ALU.add, ALU.mult).then_inc(z_ready, 1)
                if name == "gelu":
                    n = (HC // 2) * b + i_
                    dve.wait_ge(t_ready, n + 1)
                    v.scalar_tensor_tensor(gelu_u[:, n % 4, :], gelu_z[:, n % 4, :], 1.0, gelu_u[:, n % 4, :],
                                           ALU.add, ALU.mult).then_inc(h_ready, 1)
                    dve.wait_ge(h_ready, n + 1)
                    if b == 0:
                        dve.wait_ge(s_full, PAIRS * B)
                    if b == 1:
                        dve.wait_ge(*full(("kT", NT - 1, 1)))
                    if b >= 2:
                        dve.wait_ge(*full(("f2", b - 2)))
                    v.tensor_copy(h_hi[b % 2][:, 2 * i_:2 * i_ + 2, :],
                                  gelu_u[:, n % 4, :].rearrange("p (a n) -> p a n", a=2)).then_inc(h_hi_ready, 1)
                if name == "fc2":
                    dve.wait_ge(*full(("f2", b)))
                    dve.wait_ge(x2b_ready, b + 1)
                    batch = slice(TB * b, TB * b + TB)
                    gam2 = gam[:, b, C:2 * C].unsqueeze(1).to_broadcast([P, TB, C])
                    v.scalar_tensor_tensor(x2[:, batch, :], bank(("f2", b)).rearrange("p (t n) -> p t n", t=TB), 0.5,
                                           gam2, ALU.mult, ALU.mult).then_inc(ring_dve, 1)
                    dve.wait_ge(*emptied(("f2", b)))
                    v.tensor_tensor(xs[:, batch, :], x2[:, batch, :], xs[:, batch, :], ALU.add).then_inc(x3_ready, 1)
                if name == "stats2":
                    dve.wait_ge(x3_ready, b + 1)
                    statistics(2, b, xs)
                if name == "rsums1":
                    if b >= 1:
                        dve.wait_ge(rn1_ready, b)
                    for t in tiles:
                        dve.wait_ge(sq1_ready, t + 1)
                        step(v.tensor_reduce(ss[:, t % TB, 0:2 * H1], qn[:, t % TB, :].rearrange("p (h d) -> p h d", d=D1),
                                             AX.X, ALU.add))
                    if b >= 1:
                        dve.wait_ge(rope_done, TB * b)
                    seed(b, 2 * H1, v.tensor_scalar(ss[:, :, 0:2 * H1], ss[:, :, 0:2 * H1], 1e-6, None, ALU.add),
                         seed1_ready)
                if name == "rope":
                    t = TB * b + i_
                    x_ = qk[:, t % TB, :].rearrange("p (g d) -> p g d", d=D1 // 2)
                    bb = rope_b[:, t % 2, :].rearrange("p (g d) -> p g d", d=D1 // 2)
                    if t == 0:
                        dve.wait_ge(s_rope, 16)
                        dve.wait_ge(w_lo_p, 3)
                        dve.wait_ge(w_hi, 5)
                    dve.wait_ge(*emptied(("qk1", t)))
                    step(v.tensor_tensor(bb, x_, rope_sb[:, t % TB, 1:2, :].to_broadcast([P, 4 * H1, D1 // 2]), ALU.mult))
                    dve.wait_ge(cos_done, t + 1)
                    a4 = rope_a[:, t % 2, :].rearrange("p (h s d) -> p h s d", s=2, d=D1 // 2)
                    b4 = rope_b[:, t % 2, :].rearrange("p (h s d) -> p h s d", s=2, d=D1 // 2)
                    r4 = qn[:, t % TB, :].rearrange("p (h s d) -> p h s d", s=2, d=D1 // 2)
                    v.tensor_tensor(r4[:, :, 0, :], a4[:, :, 0, :], b4[:, :, 1, :], ALU.subtract)
                    step(v.tensor_tensor(r4[:, :, 1, :], a4[:, :, 1, :], b4[:, :, 0, :], ALU.add))
                    dve.wait_ge(rn1_ready, b + 1)
                    r = qn[:, t % TB, :].rearrange("p (h d) -> p h d", d=D1)
                    v.tensor_tensor(r, r, rn[:, t % TB, 0:2 * H1].unsqueeze(2).to_broadcast([P, 2 * H1, D1]), ALU.mult)\
                     .then_inc(rope_done, 1)
                if name == "lo1":
                    t = TB * b + i_
                    dve.wait_ge(stk1_hi_first, t + 1)
                    sr = stk1[:, t % TB]
                    s = sr.bitcast(F32)
                    r = qn[:, t % TB, :].rearrange("p (h d) -> p h d", d=D1)
                    v.tensor_tensor(sr[:, 0:H1, D1:2 * D1], r[:, 0:H1], s[:, 0:H1, 0:D1], ALU.subtract)
                    for i in range(2):
                        ins = v.tensor_tensor(sr[:, 2 * H1:3 * H1, i * D1:(i + 1) * D1], r[:, H1:2 * H1],
                                              s[:, H1:2 * H1, 0:D1], ALU.subtract)
                    ins.then_inc(stk1_lo, 1)
                if name == "max1":
                    for hp in range(2):
                        key = ("mx1", b, i_, hp)
                        if b >= 1 and (i_, hp) == (0, 0):
                            dve.wait_ge(sh1_ready, b)
                        dve.wait_ge(*full(key))
                        v.tensor_reduce(nm1[:, i_, 2 * hp:2 * hp + 2], bank(key).rearrange("p (h n) -> p h n", h=2),
                                        AX.X, ALU.max, negate=True).then_inc(ring_dve, 1)
                if name == "neg1":
                    dve.wait_ge(*emptied(("mx1", b, TB - 1, 1)))
                    if b >= 1:
                        dve.wait_ge(*full(("shT1", b - 1)))
                    step(v.tensor_copy(sh1[:, :, 0:H1].bitcast(F32R), nm1[:, :, :]))
                    v.tensor_tensor(sh1[:, :, H1:2 * H1].bitcast(F32R), nm1[:, :, :], sh1[:, :, 0:H1], ALU.subtract)\
                     .then_inc(sh1_ready, 1)
                if name == "shift1":
                    dve.wait_ge(*full(("shT1", b)))
                    if b == 0:
                        dve.wait_ge(const_ready, 4)
                    else:
                        dve.wait_ge(s_full, PAIRS * B + 2 * b)
                    v.tensor_copy(shs1[0:2 * H1, :], bank(("shT1", b))[0:2 * H1, 0:L]).then_inc(ring_dve, 1)
                if name == "out1":
                    key = ("sT1", b)
                    dve.wait_ge(*full(key))
                    dve.wait_ge(*emptied(("oT", B - 1, 1) if b == 0 else ("oT1", b - 1)))
                    rs = bank(key)[:, 0:TB * P].rearrange("p (t h s) -> p t h s", t=TB, h=H1)
                    v.reciprocal(rv[:, 0:TB, :], rs[:, :, :, 0]).then_inc(ring_dve, 1)
                    dve.wait_ge(*emptied(key))
                    key = ("oT1", b)
                    dve.wait_ge(*full(key))
                    dve.wait_ge(*full(("aT", B - 1) if b == 0 else ("aT1", b - 1)))
                    src = bank(key).rearrange("p (h q i d) -> p h q i d", h=2, q=TB, i=2)
                    ot = o_tok[:, :, :].rearrange("p t (h d) -> p t h d", d=D1)
                    for hp in range(2):
                        ins = v.tensor_tensor(ot[:, :, 2 * hp:2 * hp + 2, :], src[:, hp],
                                              rv[:, 0:TB, 2 * hp:2 * hp + 2].unsqueeze(3).to_broadcast([P, TB, 2, D1]),
                                              ALU.mult)
                    ins.then_inc(ring_dve, 1)
                if name == "heads1_lo":
                    split_heads(("aT1", b))
                if name == "proj1":
                    dve.wait_ge(*full(("po", b)))
                    batch = slice(TB * b, TB * b + TB)
                    v.tensor_tensor(x2[:, batch, :], bank(("po", b)).rearrange("p (t n) -> p t n", t=TB), xs[:, batch, :],
                                    ALU.add).then_inc(ring_dve, 1)


_INS = ["x", "wqkv", "wproj", "wada", "wfc1", "wfc2", "wnorm", "wqkv1", "wout1", "cols", "rows", "rope", "bias", "mask"]


def kernel(x, cond_2048, pos_BxS, mask_1x1xSxS_ff0, mask_Bx1xSxS_bf1, L0_cond_Wqkv, L0_cond_q_bias, L0_cond_v_bias,
           L0_cond_scale_mul_log, L0_cond_Wproj, L0_cond_bproj, L0_cond_Wada, L0_cond_bada, L0_cond_Wfc1, L0_cond_bfc1,
           L0_cond_Wfc2, L0_cond_bfc2, L1_cond_norm_w, L1_cond_qkv_w, L1_cond_scale, L1_cond_out_w):
    import concourse.bacc as _bacc
    from concourse.bass_utils import run_bass_kernel_spmd as _run

    def arr(a):
        return np.asarray(a)

    def columns(a, n):
        return arr(a).reshape(n, P).T

    cond = arr(cond_2048)
    cols = np.concatenate([cond.reshape(B, FC, P).transpose(2, 1, 0).reshape(P, FC * B),
                           columns(arr(L0_cond_bada)[2 * C:], 8), columns(L0_cond_bfc1, HC)], axis=1)
    rows = np.concatenate([arr(L0_cond_q_bias), np.zeros(C, np.float32), arr(L0_cond_v_bias), arr(L0_cond_bproj),
                           arr(L0_cond_bfc2), arr(L0_cond_bada)[:2 * C], arr(L0_cond_scale_mul_log).reshape(-1),
                           arr(L1_cond_scale)])[None, :]
    half = D1 // 2
    inv_freq = (np.float32(1.0) / np.float32(10000.0) ** (np.arange(half, dtype=np.float32) / np.float32(half)))
    theta = np.arange(L, dtype=np.float32)[:, None] * inv_freq.astype(np.float32)[None, :]
    rope = np.stack([np.cos(theta), np.sin(theta)], axis=1).astype(np.float32)
    given = {
        "x": arr(x).reshape(B * L, C), "wqkv": arr(L0_cond_Wqkv).T, "wproj": arr(L0_cond_Wproj).T,
        "wada": arr(L0_cond_Wada).T, "wfc1": arr(L0_cond_Wfc1).T, "wfc2": arr(L0_cond_Wfc2).T,
        "wnorm": arr(L1_cond_norm_w).T, "wqkv1": arr(L1_cond_qkv_w).T, "wout1": arr(L1_cond_out_w).T,
        "cols": cols, "rows": rows, "rope": rope, "bias": arr(mask_1x1xSxS_ff0).reshape(L, L),
        "mask": arr(mask_Bx1xSxS_bf1).reshape(B, L, L).view(np.uint8),
    }
    nc = _bacc.Bacc("TRN2", target_bir_lowering=False, num_devices=1)
    arrays, args = {}, []
    for name in _INS:
        a = np.ascontiguousarray(given[name])
        arrays[f"in_{name}"] = a
        args.append(nc.dram_tensor(f"in_{name}", a.shape, mybir.dt.from_np(a.dtype), kind="ExternalInput").ap())
    out = nc.dram_tensor("out_0", (B * L, C), F32, kind="ExternalOutput").ap()
    build(nc, *args, out)
    r = _run(nc, [arrays], core_ids=[0])
    return r.results[0]["out_0"].reshape(B, L, C)
```
